# Optimizing a Trainium2 kernel written in Bass

```python
import numpy as np
import jax
import jax.numpy as jnp

def _softmax(x, axis=-1):
    return jax.nn.softmax(x, axis=axis)

def _gelu(x):
    return jax.nn.gelu(x, approximate=True)

def _silu(x):
    return jax.nn.silu(x)

def _sigmoid(x):
    return jax.nn.sigmoid(x)

def _layernorm(x, axis=-1, eps=1e-05):
    m = jnp.mean(x, axis=axis, keepdims=True)
    v = jnp.var(x, axis=axis, keepdims=True)
    return (x - m) / jnp.sqrt(v + eps)

def _scatter_add(tgt, idx, src, axis=0):
    return tgt.at[idx].add(src)

def _segment_sum(src, seg, n):
    return jax.ops.segment_sum(src, seg, n)
kernel_name = 'mk_decoder_preln_d1_seqx_r8_4ad4c9'

def setup_inputs(seed: int=0):
    np.random.seed(seed)
    _w = jnp.asarray

    def _rec_inputs():
        import jax
        import jax.numpy as jnp
        _rk = jax.random.key(seed)
        x = 7.22e-05 + 1 * jax.random.normal(jax.random.fold_in(_rk, 1), (16, 64, 256), jnp.float32)
        _lenS = 64 - jax.random.randint(jax.random.fold_in(_rk, 7), (16,), 0, max(1, 64 // 4) + 1, jnp.int32)
        _lenS2 = 64 - jax.random.randint(jax.random.fold_in(_rk, 8), (16,), 0, max(1, 64 // 4) + 1, jnp.int32)
        _ctx_512P = jax.random.normal(jax.random.fold_in(_rk, 11), (16, 16, 64), jnp.float32)
        _ctx_512c = jax.random.dirichlet(jax.random.fold_in(_rk, 511), 0.3 * jnp.ones((16,), jnp.float32), (16, 64))
        _ctx_512t = jnp.einsum('bsk,bkd->bsd', _ctx_512c, _ctx_512P)
        _ctx_512t = _ctx_512t * jax.lax.rsqrt(jnp.mean(jnp.square(_ctx_512t)) + 1e-12) * 0.953939
        ctx_512 = -0.000514642 + 1.00011 * (_ctx_512t + 0.3 * jax.random.normal(jax.random.fold_in(_rk, 611), (16, 64, 64), jnp.float32))
        return (x, ctx_512)
    x, ctx_512 = _rec_inputs()

    def _L0_attn_setup():
        import jax, jax.numpy as jnp
        import numpy as np
        import math
        HEADS = 16
        HEAD_DIM = 128
        ROPE_BASE = 10000.0

        def _rope_tables(seq_len, head_dim):
            inv_freq = 1.0 / ROPE_BASE ** (jnp.arange(0, head_dim, 2, dtype=jnp.float32) / head_dim)
            t = jnp.arange(seq_len, dtype=jnp.float32)
            freqs = jnp.outer(t, inv_freq)
            emb = jnp.concatenate([freqs, freqs], axis=-1)
            return (jnp.cos(emb), jnp.sin(emb))

        def _rotate_half(x):
            x1, x2 = jnp.split(x, 2, axis=-1)
            return jnp.concatenate([-x2, x1], axis=-1)
        key = jax.random.key(seed)
        k1, k2, k3 = jax.random.split(key, 3)
        B, S, D = (2, 256, 256)
        x = jax.random.normal(k1, (B, S, D), dtype=jnp.float32)
        w_qkv = jax.random.normal(k2, (D, 3 * HEADS * HEAD_DIM), dtype=jnp.float32) / math.sqrt(D)
        w_out = jax.random.normal(k3, (HEADS * HEAD_DIM, D), dtype=jnp.float32) / math.sqrt(HEADS * HEAD_DIM)
        return {'x': x, 'w_qkv': w_qkv, 'w_out': w_out}
    _L0_attn_all = _L0_attn_setup()
    _L0_attn_in = {k: v for k, v in _L0_attn_all.items() if k in ('w_qkv', 'w_out')}
    del _L0_attn_all

    def _L0_xattn_setup():
        import jax, jax.numpy as jnp
        import numpy as np
        N_HEADS = 16
        N_KV_HEADS = 4
        ROPE_THETA = 10000.0
        EPS = 1e-05

        def _rms_norm(x, w):
            var = jnp.mean(x * x, axis=-1, keepdims=True)
            return x * jax.lax.rsqrt(var + EPS) * w

        def _rope_sin_cos(T, head_dim, dtype):
            inv_freq = 1.0 / ROPE_THETA ** (jnp.arange(0, head_dim, 2, dtype=jnp.float32) / head_dim)
            t = jnp.arange(T, dtype=jnp.float32)
            freqs = jnp.outer(t, inv_freq)
            emb = jnp.concatenate([freqs, freqs], -1)
            return (jnp.sin(emb).astype(dtype)[None, None], jnp.cos(emb).astype(dtype)[None, None])

        def _rotate_half(x):
            h = x.shape[-1] // 2
            x1, x2 = (x[..., :h], x[..., h:])
            return jnp.concatenate([-x2, x1], axis=-1)
        key = jax.random.key(seed)
        ks = jax.random.split(key, 6)
        B, T, C = (2, 256, 256)
        Ckv = C // N_HEADS * N_KV_HEADS
        return {'q': jax.random.normal(ks[0], (B, T, C), jnp.float32), 'k': jax.random.normal(ks[1], (B, T, Ckv), jnp.float32), 'v': jax.random.normal(ks[2], (B, T, Ckv), jnp.float32), 'q_norm_w': jnp.ones((C,), jnp.float32), 'k_norm_w': jnp.ones((Ckv,), jnp.float32), 'w_out': jax.random.normal(ks[3], (C, C), jnp.float32) * C ** (-0.5)}
    _L0_xattn_all = _L0_xattn_setup()
    _L0_xattn_in = {k: v for k, v in _L0_xattn_all.items() if k in ('q_norm_w', 'k_norm_w', 'w_out')}
    del _L0_xattn_all

    def _L0_ffn_setup():
        import jax, jax.numpy as jnp
        import numpy as np
        RANK = 64
        SCALING = 1.0 / RANK
        TEMPERATURE = 1.0
        key = jax.random.key(seed)
        k_x, k_a, k_b, k_w = jax.random.split(key, 4)
        B_, S, D = (4, 256, 256)
        E, R, O = (8, RANK, 256)
        x = jax.random.normal(k_x, (B_, S, D), dtype=jnp.float32)
        A = jax.random.normal(k_a, (E, R, D), dtype=jnp.float32) * (1.0 / np.sqrt(D))
        Bw = jax.random.normal(k_b, (E, O, R), dtype=jnp.float32) * 0.02
        Wr = jax.random.normal(k_w, (E, D), dtype=jnp.float32) * (1.0 / np.sqrt(D))
        br = jnp.zeros((E,), dtype=jnp.float32)
        return {'x': x, 'A': A, 'B': Bw, 'Wr': Wr, 'br': br}
    _L0_ffn_all = _L0_ffn_setup()
    _L0_ffn_in = {k: v for k, v in _L0_ffn_all.items() if k in ('A', 'B', 'Wr', 'br')}
    del _L0_ffn_all
    return {'x': x, 'ctx_512': ctx_512, 'L0_attn_w_qkv': _L0_attn_in['w_qkv'], 'L0_attn_w_out': _L0_attn_in['w_out'], 'L0_xattn_q_norm_w': _L0_xattn_in['q_norm_w'], 'L0_xattn_k_norm_w': _L0_xattn_in['k_norm_w'], 'L0_xattn_w_out': _L0_xattn_in['w_out'], 'L0_ffn_A': _L0_ffn_in['A'], 'L0_ffn_B': _L0_ffn_in['B'], 'L0_ffn_Wr': _L0_ffn_in['Wr'], 'L0_ffn_br': _L0_ffn_in['br']}

def reference(x, ctx_512, L0_attn_w_qkv, L0_attn_w_out, L0_xattn_q_norm_w, L0_xattn_k_norm_w, L0_xattn_w_out, L0_ffn_A, L0_ffn_B, L0_ffn_Wr, L0_ffn_br):
    import jax
    import jax.numpy as jnp

    def _L0_attn_ref(x, w_qkv, w_out):
        import jax, jax.numpy as jnp
        import numpy as np
        import math
        HEADS = 16
        HEAD_DIM = 128
        ROPE_BASE = 10000.0

        def _rope_tables(seq_len, head_dim):
            inv_freq = 1.0 / ROPE_BASE ** (jnp.arange(0, head_dim, 2, dtype=jnp.float32) / head_dim)
            t = jnp.arange(seq_len, dtype=jnp.float32)
            freqs = jnp.outer(t, inv_freq)
            emb = jnp.concatenate([freqs, freqs], axis=-1)
            return (jnp.cos(emb), jnp.sin(emb))

        def _rotate_half(x):
            x1, x2 = jnp.split(x, 2, axis=-1)
            return jnp.concatenate([-x2, x1], axis=-1)
        B, S, _ = x.shape
        scale = 1.0 / math.sqrt(HEAD_DIM)
        qkv = x @ w_qkv
        qkv = qkv.reshape(B, S, 3, HEADS, HEAD_DIM)
        q, k, v = jnp.transpose(qkv, (2, 0, 3, 1, 4))
        cos, sin = _rope_tables(S, HEAD_DIM)
        q = q * cos + _rotate_half(q) * sin
        k = k * cos + _rotate_half(k) * sin
        scores = jnp.einsum('bhid,bhjd->bhij', q, k) * scale
        causal = jnp.tril(jnp.ones((S, S), dtype=bool))
        scores = jnp.where(causal, scores, -jnp.inf)
        attn = jax.nn.softmax(scores, axis=-1)
        out = jnp.einsum('bhij,bhjd->bhid', attn, v)
        out = jnp.transpose(out, (0, 2, 1, 3)).reshape(B, S, -1)
        return out @ w_out

    def _L0_xattn_ref(q, k, v, q_norm_w, k_norm_w, w_out):
        import jax, jax.numpy as jnp
        import numpy as np
        N_HEADS = 16
        N_KV_HEADS = 4
        ROPE_THETA = 10000.0
        EPS = 1e-05

        def _rms_norm(x, w):
            var = jnp.mean(x * x, axis=-1, keepdims=True)
            return x * jax.lax.rsqrt(var + EPS) * w

        def _rope_sin_cos(T, head_dim, dtype):
            inv_freq = 1.0 / ROPE_THETA ** (jnp.arange(0, head_dim, 2, dtype=jnp.float32) / head_dim)
            t = jnp.arange(T, dtype=jnp.float32)
            freqs = jnp.outer(t, inv_freq)
            emb = jnp.concatenate([freqs, freqs], -1)
            return (jnp.sin(emb).astype(dtype)[None, None], jnp.cos(emb).astype(dtype)[None, None])

        def _rotate_half(x):
            h = x.shape[-1] // 2
            x1, x2 = (x[..., :h], x[..., h:])
            return jnp.concatenate([-x2, x1], axis=-1)
        B, T, C = q.shape
        hd = C // N_HEADS
        g = N_HEADS // N_KV_HEADS
        q = _rms_norm(q, q_norm_w)
        k = _rms_norm(k, k_norm_w)
        q = q.reshape(B, T, N_HEADS, hd).transpose(0, 2, 1, 3)
        k = k.reshape(B, T, N_KV_HEADS, hd).transpose(0, 2, 1, 3)
        v = v.reshape(B, T, N_KV_HEADS, hd).transpose(0, 2, 1, 3)
        sin, cos = _rope_sin_cos(T, hd, q.dtype)
        q = q * cos + _rotate_half(q) * sin
        k = k * cos + _rotate_half(k) * sin
        qg = q.reshape(B, N_KV_HEADS, g, T, hd)
        scale = 1.0 / jnp.sqrt(jnp.asarray(hd, q.dtype))
        scores = jnp.einsum('bgnqd,bgkd->bgnqk', qg, k) * scale
        causal = jnp.tril(jnp.ones((T, T), bool))
        scores = jnp.where(causal, scores, jnp.asarray(-1e+30, scores.dtype))
        attn = jax.nn.softmax(scores, axis=-1)
        out = jnp.einsum('bgnqk,bgkd->bgnqd', attn, v)
        out = out.reshape(B, N_HEADS, T, hd).transpose(0, 2, 1, 3).reshape(B, T, C)
        return out @ w_out.T

    def _L0_ffn_ref(x, A, B, Wr, br):
        import jax, jax.numpy as jnp
        import numpy as np
        RANK = 64
        SCALING = 1.0 / RANK
        TEMPERATURE = 1.0
        batch, seq, d = x.shape
        E, out_dim = (B.shape[0], B.shape[1])
        x_flat = x.reshape(-1, d)
        logits = (x_flat @ Wr.T + br) / TEMPERATURE
        probs = jax.nn.softmax(logits, axis=-1)
        expert_idx = jnp.argmax(probs, axis=-1)
        expert_weight = jnp.max(probs, axis=-1)
        h = jnp.einsum('nd,erd->ner', x_flat, A)
        y = jnp.einsum('ner,eor->neo', h, B) * SCALING
        sel = jnp.take_along_axis(y, expert_idx[:, None, None], axis=1)[:, 0, :]
        out_flat = sel * expert_weight[:, None]
        return out_flat.reshape(batch, seq, out_dim)
    x = x + _L0_attn_ref(_layernorm(x, axis=-1), L0_attn_w_qkv, L0_attn_w_out)
    x = x + _L0_xattn_ref(_layernorm(x, axis=-1), ctx_512, ctx_512, L0_xattn_q_norm_w, L0_xattn_k_norm_w, L0_xattn_w_out)
    x = x + _L0_ffn_ref(_layernorm(x, axis=-1), L0_ffn_A, L0_ffn_B, L0_ffn_Wr, L0_ffn_br)
    return x

_drawn_inputs = setup_inputs


def setup_inputs(seed=0):
    import zlib

    import numpy as np

    out = dict(_drawn_inputs(seed))
    spreads = {'L0_xattn_q_norm_w': (1.0, 0.2), 'L0_xattn_k_norm_w': (1.0, 0.2), 'L0_ffn_br': (0.0, 0.8)}
    factors = {'L0_ffn_A': 8.0, 'L0_ffn_B': 8.0, 'L0_ffn_Wr': 8.0}
    for name, (base, spread) in spreads.items():
        noise = np.random.default_rng([zlib.crc32(name.encode()), seed]).standard_normal(out[name].shape)
        drawn = base * np.exp(spread * noise) if base else spread * noise
        out[name] = jnp.asarray(drawn.astype(out[name].dtype))
    for name, factor in factors.items():
        out[name] = (out[name] * factor).astype(out[name].dtype)
    return out
```

```python
from contextlib import ExitStack

import numpy as np

import concourse.bass as bass
from concourse import mybir

ALU = mybir.AluOpType
ACT = mybir.ActivationFunctionType
AX_X = mybir.AxisListType.X
F32 = mybir.dt.float32
F32R = mybir.dt.float32r
BF16 = mybir.dt.bfloat16

P = 128
B, S, D = 16, 64, 256
TILES = B * S // P
KC = D // P
CHUNKS = 2
CT = TILES // CHUNKS
CN = CT * P
HEADS, HD = 16, 128
PAIRS = HEADS // 2
XH, XD = 16, 16
XG = 4
XC = XG * XD
HH = XH // KC
E, R = 8, 64
EM = E * R // P
EPS = 1e-5
NEG = -1e30

_COLS = {}
_at = 0
for _name, _n in (("ident", P), ("mask", P), ("xmask", S), ("cosq", S), ("sinq", S), ("cosk", S), ("sink", S),
                  ("xcosq", XD), ("xsinq", XD), ("xcosk", XD), ("xsink", XD), ("first", E)):
    _COLS[_name] = (_at, _at + _n)
    _at += _n
CONST_N = _at


def rope_tables(positions, width):
    inv = (1.0 / 10000.0 ** (np.arange(0, width, 2, dtype=np.float32) / np.float32(width))).astype(np.float32)
    freqs = np.outer(np.arange(positions, dtype=np.float32), inv).astype(np.float32)
    emb = np.concatenate([freqs, freqs], -1)
    sin = np.sin(emb).astype(np.float32)
    sin[:, : width // 2] *= -1.0
    return np.cos(emb).astype(np.float32), sin


def constants():
    c = np.zeros((P, CONST_N), np.float32)

    def put(name, a):
        lo, hi = _COLS[name]
        c[:, lo:hi] = a

    put("ident", np.eye(P))
    p, j = np.arange(P)[:, None], np.arange(P)[None, :]
    put("mask", np.where((p // S == j // S) & (j <= p), 0.0, NEG))
    put("xmask", np.where(np.arange(S)[None, :] <= p % S, 0.0, NEG))
    cos, sin = rope_tables(S, HD)
    scale = np.float32(HD) ** np.float32(-0.5)
    put("cosq", cos.T * scale)
    put("sinq", sin.T * scale)
    put("cosk", cos.T)
    put("sink", sin.T)
    cos, sin = rope_tables(S, XD)
    cos, sin = np.tile(cos, (2, 1)), np.tile(sin, (2, 1))
    scale = np.float32(XD) ** np.float32(-0.5)
    put("xcosq", cos * scale)
    put("xsinq", sin * scale)
    put("xcosk", cos)
    put("xsink", sin)
    put("first", np.arange(E, 0, -1)[None, :])
    return c


def decoder_kernel(nc, x, ctx_in, w_qkv, w_o, q_norm_w, k_norm_w, wx_o, ffn_a, ffn_b, ffn_wr, ffn_br, consts, out):
    x_v = x.rearrange("b s d -> (b s) d").rearrange("(t p) d -> p t d", p=P)
    out_v = out.rearrange("b s d -> (b s) d").rearrange("(t p) d -> p t d", p=P)
    ctx_v = ctx_in.rearrange("b s d -> (b s) d").rearrange("(t p) d -> p t d", p=P)
    wqkv_v = w_qkv.rearrange("(k p) (w n) -> p k w n", p=P, w=3)
    wo_v = w_o.rearrange("(h p) n -> p h n", p=P)

    with ExitStack() as stack:
        def sb(name, shape, dt=F32):
            return stack.enter_context(nc.sbuf_tensor(name, shape, dt))

        def sem(name):
            return stack.enter_context(nc.semaphore(name))

        bank = [stack.enter_context(nc.psum_tensor(f"bank{i}", [P, 512], F32)) for i in range(8)]

        cst = sb("cst", [P, CONST_N])
        identb = sb("identb", [P, P], BF16)
        xmaskb = sb("xmaskb", [P, S], BF16)
        mhalf = sb("mhalf", [P, 16])
        xr = sb("xr", [P, TILES, D])
        xn = sb("xn", [P, TILES, D])
        bn6 = sb("bn6", [P, TILES, 6])
        bn2 = sb("bn2", [P, TILES, 2])
        veps = sb("veps", [P, TILES])
        rstd = sb("rstd", [P, TILES])
        cx = sb("cx", [P, TILES, XC])
        cssq = sb("cssq", [P, TILES])
        crr = sb("crr", [P, TILES])
        kw_bc = sb("kw_bc", [P, XC])
        qw_bc = sb("qw_bc", [P, D])
        kT = sb("kT", [XC, B, S])
        kblk = sb("kblk", [P, KC, B, HH, S])
        vblk = sb("vblk", [P, B, XG, 2 * XD])
        ssq = sb("ssq", [P, TILES])
        rr = sb("rr", [P, TILES])
        wxoT = sb("wxoT", [P, KC, D])
        aT = sb("aT", [P, KC, E * R])
        bT = sb("bT", [P, EM, D])
        wrT = sb("wrT", [P, KC, E])
        br_bc = sb("br_bc", [P, E])

        main_mem = ExitStack()

        def sbm(name, shape, dt=F32):
            return main_mem.enter_context(nc.sbuf_tensor(name, shape, dt))

        xT_hi = sbm("xT_hi", [P, KC, TILES * P], F32R)
        xT_lo = sbm("xT_lo", [P, KC, TILES * P], F32R)
        w_st = sbm("w_st", [P, KC, 3, 2 * HD])
        wo_st = sbm("wo_st", [P, 2, D])
        wqk_hi = [sbm(f"wqk_hi{h}", [P, KC, 2, HD], F32R) for h in range(2)]
        wqk_lo = [sbm(f"wqk_lo{h}", [P, KC, 2, HD], F32R) for h in range(2)]
        wv_hi = sbm("wv_hi", [P, KC, 2 * HD], F32R)
        wv_lo = sbm("wv_lo", [P, KC, 2 * HD], F32R)
        wo_hi = sbm("wo_hi", [P, 2, D], F32R)
        wo_lo = sbm("wo_lo", [P, 2, D], F32R)
        swapped = [sbm(f"swapped{i}", [P, CN]) for i in range(2)]
        cos_t = [sbm(f"cos_t{i}", [P, CN]) for i in range(2)]
        sin_t = [sbm(f"sin_t{i}", [P, CN]) for i in range(2)]
        qk = [[sbm(f"qk{h}{i}", [P, CN]) for i in range(2)] for h in range(2)]
        masked = [sbm(f"masked{h}", [P, CT, P]) for h in range(2)]
        nmax = [sbm(f"nmax{h}", [P, CT]) for h in range(2)]
        expd = [sbm(f"expd{h}", [P, CT, P]) for h in range(2)]
        rsum = [sbm(f"rsum{h}", [P, CT]) for h in range(2)]
        rrec = [sbm(f"rrec{h}", [P, CT]) for h in range(2)]
        probs = [sbm(f"probs{h}", [P, CT, P]) for h in range(2)]
        probsT = sbm("probsT", [P, CT, P])
        vals = [sbm(f"vals{c}", [P, CT, 2 * HD]) for c in range(2)]
        with ExitStack() as early:
            cx2 = early.enter_context(nc.sbuf_tensor("cx2", [P, B, XC], F32))
            wst2 = early.enter_context(nc.sbuf_tensor("wst2", [P, KC, D], F32))
            wr_st = early.enter_context(nc.sbuf_tensor("wr_st", [E, D], F32))
        ao_hi = [[sbm(f"ao_hi{c}{h}", [P, CN], F32R) for h in range(2)] for c in range(2)]
        ao_lo = [[sbm(f"ao_lo{c}{h}", [P, CN], F32R) for h in range(2)] for c in range(2)]

        main_mem.close()
        xq_t = [sb(f"xq{c}", [P, CT, D]) for c in range(2)]

        xcos_t = [sb(f"xcos{c}", [P, CT, D]) for c in range(2)]

        def xq(c):
            return xq_t[c][:, :, :]

        def xcos(c):
            return xcos_t[c][:, :, :]

        def xsin(c):
            return xn[:, c * CT:(c + 1) * CT, :]
        qT = [sb(f"qT{c}", [P, CT, KC, P]) for c in range(2)]
        xsc_t = [sb(f"xsc{i}", [P, XH, S]) for i in range(2)]
        xprobs_t = [sb(f"xprobs{i}", [P, XH, S]) for i in range(2)]
        xmx_t = [sb(f"xmx{i}", [P, XH]) for i in range(2)]
        xsm_t = [sb(f"xsm{i}", [P, XH]) for i in range(2)]
        xrec_t = [sb(f"xrec{i}", [P, XH]) for i in range(2)]
        xpT_t = [sb(f"xpT{i}", [P, HH, P]) for i in range(1)]
        xaoT_t = [sb(f"xaoT{i}", [P, KC, P]) for i in range(2)]

        def xexp(t):
            return xsc_t[t % 2][:, :, :]

        def xprobs(t):
            return xprobs_t[t % 2][:, :, :]

        def xrec(t):
            return xrec_t[t % 2][:, :]
        fT = [sb(f"fT{c}", [P, KC, CN]) for c in range(2)]
        fmask = sb("fmask", [P, EM, CN], BF16)
        fhm = sb("fhm", [P, EM, CN])
        lg = sb("lg", [P, 12, CT * E])
        lgs = sb("lgs", [P, 8, CT])
        onehot = [sb(f"onehot{c}", [P, CT * E], BF16) for c in range(2)]
        chosen = sb("chosen", [P, CT * E * R], BF16)
        wgt = [sb(f"wgt{c}", [P, CT]) for c in range(2)]
        final = sb("final", [P, TILES, D])


        rows_loaded = sem("rows_loaded")
        cssq_done = sem("cssq_done")
        crr_done = sem("crr_done")
        lshift_done = sem("lshift_done")
        consts_loaded = sem("consts_loaded")
        w_loaded = sem("w_loaded")
        wo_loaded = sem("wo_loaded")
        small_loaded = sem("small_loaded")
        ctx_loaded = sem("ctx_loaded")
        kblk_loaded = sem("kblk_loaded")
        out_stored = sem("out_stored")
        dve_step = sem("dve_step")
        pool_step = sem("pool_step")
        var_done = sem("var_done")
        rstd_done = sem("rstd_done")
        xn_done = sem("xn_done")
        xT_ps_done = sem("xT_ps_done")
        xT_hi_done = sem("xT_hi_done")
        xT_lo_done = sem("xT_lo_done")
        wqk_hi_done = sem("wqk_hi_done")
        wqk_lo_done = sem("wqk_lo_done")
        wv_hi_done = sem("wv_hi_done")
        wv_lo_done = sem("wv_lo_done")
        wo_hi_done = sem("wo_hi_done")
        wo_lo_done = sem("wo_lo_done")
        scores_done = sem("scores_done")
        mask_done = sem("mask_done")
        max_done = sem("max_done")
        exp_done = sem("exp_done")
        recip_done = sem("recip_done")
        probs_done = sem("probs_done")
        probsT_ps_done = sem("probsT_ps_done")
        probsT_done = sem("probsT_done")
        v_done = sem("v_done")
        v_copied = sem("v_copied")
        av_done = sem("av_done")
        ao_hi_done = sem("ao_hi_done")
        ao_lo_done = sem("ao_lo_done")
        out_done = sem("out_done")
        out_added = sem("out_added")
        prep_ps_done = sem("prep_ps_done")
        prep_copied = sem("prep_copied")
        cons_done = sem("cons_done")
        kn_done = sem("kn_done")
        kT_ready = sem("kT_ready")
        kblk_zeroed = sem("kblk_zeroed")
        vblk_ready = sem("vblk_ready")
        xvar_done = sem("xvar_done")
        xrstd_done = sem("xrstd_done")
        xln_done = sem("xln_done")
        xssq_done = sem("xssq_done")
        xssqe_done = sem("xssqe_done")
        xrr_done = sem("xrr_done")
        xq_cos = sem("xq_cos")
        xq_sin = sem("xq_sin")
        xq_done = sem("xq_done")
        xqT_ps_done = sem("xqT_ps_done")
        xqT_copied = sem("xqT_copied")
        xsc_done = sem("xsc_done")
        xmax_done = sem("xmax_done")
        xsub_done = sem("xsub_done")
        xexp_done = sem("xexp_done")
        xsum_done = sem("xsum_done")
        xprobs_done = sem("xprobs_done")
        xpT_ps_done = sem("xpT_ps_done")
        xpT_copied = sem("xpT_copied")
        xav_done = sem("xav_done")
        xao_copied = sem("xao_copied")
        xproj_done = sem("xproj_done")
        x2_done = sem("x2_done")
        fvar_done = sem("fvar_done")
        frstd_done = sem("frstd_done")
        fln_done = sem("fln_done")
        fT_ps_done = sem("fT_ps_done")
        fT_copied = sem("fT_copied")
        logits_done = sem("logits_done")
        fh_done = sem("fh_done")
        fexp_done = sem("fexp_done")
        onehot_done = sem("onehot_done")
        chosen_done = sem("chosen_done")
        fmask_done = sem("fmask_done")
        fmask_copied = sem("fmask_copied")
        fhm_done = sem("fhm_done")
        y_done = sem("y_done")
        final_done = sem("final_done")
        x_loaded = [sem(f"x_loaded{c}") for c in range(CHUNKS)]
        qk_cos = [sem("q_cos"), sem("k_cos")]
        qk_done = [sem("q_done"), sem("k_done")]
        qk_roped = [sem("q_roped"), sem("k_roped")]
        qk_sin = [sem("q_sin"), sem("k_sin")]
        qk_swapped = [sem("q_swapped"), sem("k_swapped")]
        block = stack.enter_context(nc.Block())

        def C(name, rows=slice(0, P)):
            lo, hi = _COLS[name]
            return cst[rows, lo:hi]

        ident = C("ident")
        split3 = [(0, 0), (0, 1), (1, 0)]
        xT = (xT_hi, xT_lo)
        wqk = (wqk_hi, wqk_lo)
        wv = (wv_hi, wv_lo)
        wo = (wo_hi, wo_lo)
        ao = (ao_hi, ao_lo)
        BQ, BK, BS, BT_, BAV, BW0, BW1, BP = bank

        def needed(value):
            return not isinstance(value, int) or value > 0

        def has(mode, u, lag):
            if mode == "first":
                return u - lag >= 0
            if mode == "last":
                return u - lag < 0
            return True

        @block.sync
        def _(sp):
            for c in range(CHUNKS):
                sp.dma_start(xr[:, c * CT:(c + 1) * CT, :], x_v[:, c * CT:(c + 1) * CT, :]).then_inc(x_loaded[c], 16)
            sp.dma_start(cst[:, :], consts).then_inc(consts_loaded, 16)

            def load_w(i):
                for w in range(3):
                    sp.dma_start(w_st[:, :, w, :], wqkv_v[:, :, w, bass.ds(i * 2 * HD, 2 * HD)]).then_inc(w_loaded, 16)

            def load_wo(i):
                sp.dma_start(wo_st[:, :, :], wo_v[:, bass.ds(i * 2, 2), :]).then_inc(wo_loaded, 16)

            load_w(0)
            load_wo(0)
            sp.dma_start(cx[:, :, :], ctx_v).then_inc(ctx_loaded, 16)
            for half in range(2):
                sp.dma_start(cx2[half * S:(half + 1) * S, :, :], ctx_in.rearrange("b s d -> s b d")).then_inc(ctx_loaded, 16)
            small, rows = small_loaded, rows_loaded
            sp.dma_start(kw_bc[:, :], k_norm_w.rearrange("(a n) -> a n", a=1).to_broadcast([P, XC])).then_inc(rows, 16)
            sp.dma_start(qw_bc[:, :], q_norm_w.rearrange("(a n) -> a n", a=1).to_broadcast([P, D])).then_inc(rows, 16)
            sp.dma_start(br_bc[:, :], ffn_br.rearrange("(a n) -> a n", a=1).to_broadcast([P, E])).then_inc(rows, 16)
            sp.dma_start(wr_st[:, :], ffn_wr).then_inc(small, 16)
            sp.dma_start(wst2[:, 0:2, :], wx_o.rearrange("(k p) c -> p k c", p=P)).then_inc(small, 16)
            sp.wait_ge(xT_ps_done, 2 * TILES)
            sp.dma_start(xn[:, 0:4, :], ffn_a.rearrange("e r d -> (e r) d").rearrange("(m p) d -> p m d", p=P)).then_inc(small, 16)
            for k in range(KC):
                sp.dma_start(xn[:, 4 + 2 * k:6 + 2 * k, :].rearrange("p t (e r) -> p (t e) r", r=R),
                             ffn_b[:, k * P:(k + 1) * P, :].rearrange("e o r -> o e r")).then_inc(small, 16)
            with sp.Fori(1, PAIRS) as i:
                sp.wait_ge(wqk_hi_done, i * 2)
                sp.wait_ge(wqk_lo_done, i * 2)
                sp.wait_ge(wv_hi_done, i)
                sp.wait_ge(wv_lo_done, i)
                load_w(i)
                sp.wait_ge(wo_hi_done, i)
                sp.wait_ge(wo_lo_done, i)
                load_wo(i)
            sp.wait_ge(kblk_zeroed, 2)
            sp.wait_ge(prep_copied, 2)
            for h in range(XH):
                k, hh, g = h // HH, h % HH, h // (XH // XG)
                sp.dma_start(kblk[hh * XD:(hh + 1) * XD, k, :, hh, :], kT[g * XD:(g + 1) * XD, :, :]).then_inc(kblk_loaded, 16)
            for t in range(TILES):
                sp.wait_ge(final_done, t + 1)
                sp.dma_start(out_v[:, t, :], final[:, t, :]).then_inc(out_stored, 16)
            sp.wait_ge(out_stored, 16 * TILES)

        @block.gpsimd
        def _(pool):
            pool.memset(mhalf[:, :], -0.5).then_inc(pool_step, 1)
            pool.memset(kblk[:, 0, :, :, :], 0.0).then_inc(kblk_zeroed, 1)
            pool.wait_ge(pool_step, 1)

            for c in range(CHUNKS):
                pool.wait_ge(var_done, c + 1)
                pool.tensor_tensor(rstd[:, c * CT:(c + 1) * CT], veps[:, c * CT:(c + 1) * CT], mhalf[:, 0:CT], ALU.pow).then_inc(rstd_done, 1)

            def lo_qk(h, it):
                pool.wait_ge(wqk_hi_done, it * 2 + h + 1)
                if needed(it):
                    pool.wait_ge(qk_done[1], it * 4 - 1 + h)
                pool.tensor_tensor(wqk_lo[h][:, :, :, :], w_st[:, :, 0:2, h * HD:(h + 1) * HD], wqk_hi[h][:, :, :, :].bitcast(F32), ALU.subtract).then_inc(wqk_lo_done, 1)

            def lo_v(it):
                pool.wait_ge(wv_hi_done, it + 1)
                pool.tensor_tensor(wv_lo[:, :, :], w_st[:, :, 2, :], wv_hi[:, :, :].bitcast(F32), ALU.subtract).then_inc(wv_lo_done, 1)

            def lo_o(it):
                pool.wait_ge(wo_hi_done, it + 1)
                pool.tensor_tensor(wo_lo[:, :, :], wo_st[:, :, :], wo_hi[:, :, :].bitcast(F32), ALU.subtract).then_inc(wo_lo_done, 1)

            lo_qk(0, 0)
            pool.wait_ge(cssq_done, 1)
            pool.tensor_tensor(crr[:, :], cssq[:, :], mhalf[:, 0:TILES], ALU.pow).then_inc(crr_done, 1)
            pool.memset(vblk[:, :, :, :], 0.0).then_inc(pool_step, 1)
            pool.wait_ge(pool_step, 2)
            pool.wait_ge(ctx_loaded, 48)
            for half in range(2):
                rows = slice(half * S, (half + 1) * S)
                pool.tensor_copy(vblk[rows, :, :, half * XD:(half + 1) * XD],
                                 cx2[rows, :, :].rearrange("p b (g d) -> p b g d", g=XG)).then_inc(vblk_ready, 1)
                pool.wait_ge(vblk_ready, half + 1)

            def rope_add(it, u):
                h, n = u % 2, it * 4 + u
                for i in range(2):
                    pool.wait_ge(qk_sin[i], n + 1)
                    if i == 0:
                        if needed(n - 1):
                            pool.wait_ge(scores_done, n - 1)
                    pool.tensor_tensor(qk[h][i][:, :], cos_t[i][:, :], sin_t[i][:, :], ALU.add).then_inc(qk_roped[i], 1)

            def normalise(it, u):
                h, n = (u - 1) % 2, it * 4 + u - 1
                pool.wait_ge(recip_done, n + 1)
                if needed(n - 1):
                    pool.wait_ge(probsT_ps_done, n - 1)
                pool.tensor_tensor(probs[h][:, :, :], expd[h][:, :, :],
                                   rrec[h][:, :].unsqueeze(2).to_broadcast([P, CT, P]), ALU.mult).then_inc(probs_done, 1)

            def iteration(it, mode):
                for u in range(4):
                    if has(mode, u, 0) and mode != "last":
                        if u == 0:
                            lo_qk(1, it)
                            lo_v(it)
                        if u == 3:
                            lo_o(it)
                            if mode != "end":
                                lo_qk(0, it + 1)
                        rope_add(it, u)
                    if has(mode, u, 1):
                        normalise(it, u)

            iteration(0, "first")
            with pool.Fori(1, PAIRS - 1) as it:
                iteration(it, "loop")
            iteration(PAIRS - 1, "end")
            iteration(PAIRS, "last")

            for c in range(CHUNKS):
                cs = slice(c * CT, (c + 1) * CT)
                pool.wait_ge(xvar_done, c + 1)
                pool.tensor_tensor(rstd[:, cs], veps[:, cs], mhalf[:, 0:CT], ALU.pow).then_inc(xrstd_done, 1)
            for c in range(CHUNKS):
                cs = slice(c * CT, (c + 1) * CT)
                pool.wait_ge(xssqe_done, c + 1)
                pool.tensor_tensor(rr[:, cs], ssq[:, cs], mhalf[:, 0:CT], ALU.pow).then_inc(xrr_done, 1)
                pool.wait_ge(xq_sin, c + 1)
                pool.tensor_tensor(xq(c), xcos(c), xsin(c), ALU.add).then_inc(xq_done, 1)
            for t in range(TILES):
                pool.wait_ge(xsum_done, t + 1)
                if needed(t - 1):
                    pool.wait_ge(xpT_ps_done, t - 1)
                pool.tensor_tensor(xprobs(t), xexp(t), xrec(t).unsqueeze(2).to_broadcast([P, XH, S]), ALU.mult).then_inc(xprobs_done, 1)
            for c in range(CHUNKS):
                cs = slice(c * CT, (c + 1) * CT)
                pool.wait_ge(fvar_done, c + 1)
                pool.tensor_tensor(rstd[:, cs], veps[:, cs], mhalf[:, 0:CT], ALU.pow).then_inc(frstd_done, 1)

        @block.scalar
        def _(act):
            def hi_qk(h, it):
                act.wait_ge(w_loaded, it * 48 + 48)
                if needed(it):
                    act.wait_ge(qk_done[1], it * 4 - 1 + h)
                    act.wait_ge(wqk_lo_done, it * 2 - 1 + h)
                act.activation(wqk_hi[h][:, :, :, :], w_st[:, :, 0:2, h * HD:(h + 1) * HD], ACT.Copy).then_inc(wqk_hi_done, 1)

            def hi_v(it):
                if needed(it):
                    act.wait_ge(v_done, it * 2)
                    act.wait_ge(wv_lo_done, it)
                act.activation(wv_hi[:, :, :], w_st[:, :, 2, :], ACT.Copy).then_inc(wv_hi_done, 1)

            def hi_o(it):
                act.wait_ge(wo_loaded, it * 16 + 16)
                if needed(it):
                    act.wait_ge(out_done, it * 2)
                    act.wait_ge(wo_lo_done, it)
                act.activation(wo_hi[:, :, :], wo_st[:, :, :], ACT.Copy).then_inc(wo_hi_done, 1)

            for t in range(TILES):
                act.wait_ge(xT_ps_done, 2 * t + 2)
                act.activation(xT_hi[:, :, t * P:(t + 1) * P], bank[2 + t % 2][:, 0:D].rearrange("p (k n) -> p k n", k=KC), ACT.Copy).then_inc(xT_hi_done, 1)
                if t == 3:
                    hi_qk(0, 0)

            def swap(it, u):
                n = it * 4 + u
                for i, bk in enumerate((BQ, BK)):
                    act.wait_ge(qk_done[i], n + 1)
                    if needed(n):
                        act.wait_ge(qk_sin[i], n)
                    act.activation(swapped[i][0:S, :], bk[S:P, :], ACT.Copy)
                    act.activation(swapped[i][S:P, :], bk[0:S, :], ACT.Copy).then_inc(qk_swapped[i], 1)

            def exponentials(it, u):
                h, n = (u - 1) % 2, it * 4 + u - 1
                act.wait_ge(max_done, n + 1)
                if needed(n - 1):
                    act.wait_ge(probs_done, n - 1)
                for t in range(CT):
                    i = act.activation(expd[h][:, t, :], masked[h][:, t, :], ACT.Exp, bias=nmax[h][:, t:t + 1],
                                       scale=1.0, accum_out=rsum[h][:, t:t + 1])
                i.then_inc(exp_done, 1)

            def copy_probsT(it, u):
                n = it * 4 + u - 2
                act.wait_ge(probsT_ps_done, n + 1)
                if needed(n):
                    act.wait_ge(av_done, n)
                act.activation(probsT[:, :, :], BT_[:, :].rearrange("p (t n) -> p t n", t=CT), ACT.Copy).then_inc(probsT_done, 1)

            def copy_v(it, c):
                act.wait_ge(v_done, it * 2 + c + 1)
                if needed(it):
                    act.wait_ge(av_done, it * 4 - 2 + 2 * c)
                act.activation(vals[c][:, 0:2, :], BW0[:, :].rearrange("p (t n) -> p t n", t=2), ACT.Copy)
                act.activation(vals[c][:, 2:4, :], BW1[:, :].rearrange("p (t n) -> p t n", t=2), ACT.Copy).then_inc(v_copied, 1)

            def ao_high(it, u):
                n, c, h = it * 4 + u - 2, ((u - 2) % 4) // 2, u % 2
                act.wait_ge(av_done, n + 1)
                act.activation(ao_hi[c][h][:, :], BAV[:, :], ACT.Copy).then_inc(ao_hi_done, 1)

            def iteration(it, mode):
                for u in range(4):
                    live = mode != "last"
                    if live and u == 0:
                        hi_qk(1, it)
                        hi_v(it)
                    if live and u == 3:
                        hi_o(it)
                        if mode != "end":
                            hi_qk(0, it + 1)
                    if live:
                        swap(it, u)
                    if has(mode, u, 2):
                        copy_probsT(it, u)
                    if has(mode, u, 1):
                        exponentials(it, u)
                    if live and u % 2:
                        copy_v(it, u // 2)
                    if has(mode, u, 2):
                        ao_high(it, u)

            iteration(0, "first")
            with act.Fori(1, PAIRS - 1) as it:
                iteration(it, "loop")
            iteration(PAIRS - 1, "end")
            iteration(PAIRS, "last")

            def cross_tail(t):
                act.wait_ge(xpT_ps_done, t + 1)
                if needed(t):
                    act.wait_ge(xav_done, t)
                for k in range(2):
                    i = act.activation(xpT_t[0][:, 4 * k:4 * k + 4, :], bank[4 + k][:, :].rearrange("p (m n) -> p m n", m=4), ACT.Copy)
                i.then_inc(xpT_copied, 1)
                act.wait_ge(xav_done, t + 1)
                if needed(t - 1):
                    act.wait_ge(xproj_done, t - 1)
                act.activation(xaoT_t[t % 2][:, :, :], bank[6][:, 0:KC * P].rearrange("p (k n) -> p k n", k=KC), ACT.Copy).then_inc(xao_copied, 1)

            for c in range(CHUNKS):
                act.wait_ge(xln_done, c + 1)
                for t in range(c * CT, (c + 1) * CT):
                    i = act.activation(xq_t[c][:, t % CT, :], xn[:, t, :], ACT.Square, accum_out=ssq[:, t:t + 1])
                i.then_inc(xssq_done, 1)

            def copy_qT(c):
                act.wait_ge(xqT_ps_done, c + 1)
                for k in range(2):
                    i = act.activation(qT[c][:, 2 * k:2 * k + 2, :, :],
                                       bank[4 + k][:, :].rearrange("p (t k n) -> p t k n", t=2, k=KC), ACT.Copy)
                i.then_inc(xqT_copied, 1)

            copy_qT(0)
            for t in range(TILES):
                act.wait_ge(xsub_done, t + 1)
                act.activation(xexp(t), xexp(t), ACT.Exp).then_inc(xexp_done, 1)
                if t:
                    cross_tail(t - 1)
                if t == CT - 1:
                    copy_qT(1)
            cross_tail(TILES - 1)

            for c in range(CHUNKS):
                act.wait_ge(fT_ps_done, c + 1)
                for k in range(KC):
                    i = act.activation(fT[c][:, k, :], bank[4 + k][:, :], ACT.Copy)
                i.then_inc(fT_copied, 1)
                act.wait_ge(lshift_done, c + 1)
                act.activation(lg[:, 2, :], lg[:, 1, :], ACT.Exp).then_inc(fexp_done, 1)
                act.wait_ge(onehot_done, c + 1)
                if needed(EM * c):
                    act.wait_ge(fmask_done, EM * c)
                act.activation(chosen[:, :].rearrange("p (n r) -> p n r", r=R), onehot[c][:, :].unsqueeze(2).to_broadcast([P, CT * E, R]), ACT.Copy).then_inc(chosen_done, 1)
                for m in range(EM):
                    act.wait_ge(fmask_done, EM * c + m + 1)
                    if needed(EM * (c - 1) + m + 1):
                        act.wait_ge(fhm_done, EM * (c - 1) + m + 1)
                    act.activation(fmask[:, m, :], bank[6 + m % 2][:, :], ACT.Copy).then_inc(fmask_copied, 1)

        def prep_list():
            todo = [(kT[:, :, :].rearrange("p b n -> p (b n)")[:, t * P:(t + 1) * P], cx[:, t, :], XC, P) for t in range(TILES)]
            for k in range(KC):
                for h in range(KC):
                    todo.append((wxoT[:, h, k * P:(k + 1) * P], wst2[:, k, h * P:(h + 1) * P], P, P))
            for k in range(KC):
                todo.append((wrT[:, k, :], wr_st[:, k * P:(k + 1) * P], P, E))
            for m in range(EM):
                for k in range(KC):
                    todo.append((aT[:, k, m * P:(m + 1) * P], xn[:, m, k * P:(k + 1) * P], P, P))
            for k in range(KC):
                for m in range(EM):
                    src = xn[:, 4 + 2 * k:6 + 2 * k, :].rearrange("p t n -> p (t n)")[:, m * P:(m + 1) * P]
                    todo.append((bT[:, m, k * P:(k + 1) * P], src, P, P))
            return todo

        SMALL_ALL = 16 * 5
        PREP = prep_list()

        @block.tensor
        def _(pe):
            pe.wait_ge(consts_loaded, 16)
            for t in range(TILES):
                pe.wait_ge(xn_done, t + 1)
                if needed(t - 1):
                    pe.wait_ge(xT_lo_done, t - 1)
                for k in range(KC):
                    pe.transpose(bank[2 + t % 2][:, k * P:(k + 1) * P], xn[:, t, k * P:(k + 1) * P], ident).then_inc(xT_ps_done, 1)
            def project_qk(it, u):
                c, h, n = u // 2, u % 2, it * 4 + u
                if c == 0:
                    pe.wait_ge(wqk_hi_done, it * 2 + h + 1)
                    pe.wait_ge(wqk_lo_done, it * 2 + h + 1)
                for i, bk in enumerate((BQ, BK)):
                    if needed(n):
                        pe.wait_ge(qk_cos[i], n)
                    for j, (a, b) in enumerate(split3):
                        for k in range(KC):
                            mm = pe.matmul(bk[:, :], wqk[a][h][:, k, i, :], xT[b][:, k, c * CN:(c + 1) * CN],
                                           start=(j == 0 and k == 0), stop=(j == 2 and k == KC - 1))
                    mm.then_inc(qk_done[i], 1)

            def scores(it, u):
                h, n = (u - 1) % 2, it * 4 + u - 1
                pe.wait_ge(qk_roped[1], n + 1)
                if needed(n):
                    pe.wait_ge(mask_done, n)
                for t in range(CT):
                    cols = slice(t * P, (t + 1) * P)
                    mm = pe.matmul(BS[:, cols], qk[h][0][:, cols], qk[h][1][:, cols], start=True, stop=True)
                mm.then_inc(scores_done, 1)

            def transpose_probs(it, u):
                h, n = u % 2, it * 4 + u - 2
                pe.wait_ge(probs_done, n + 1)
                if needed(n):
                    pe.wait_ge(probsT_done, n)
                for t in range(CT):
                    mm = pe.transpose(BT_[:, t * P:(t + 1) * P], probs[h][:, t, :], ident)
                mm.then_inc(probsT_ps_done, 1)

            def attend(it, u):
                h, c, n = u % 2, ((u - 2) % 4) // 2, it * 4 + u - 2
                pe.wait_ge(probsT_done, n + 1)
                pe.wait_ge(v_copied, 2 * it + c + 1 if u >= 2 else 2 * it - 1 + c)
                if needed(n):
                    pe.wait_ge(ao_lo_done, n)
                for t in range(CT):
                    mm = pe.matmul(BAV[:, t * P:(t + 1) * P], vals[c][:, t, h * HD:(h + 1) * HD], probsT[:, t, :], start=True, stop=True)
                mm.then_inc(av_done, 1)

            def project_v(it, c):
                if c == 0:
                    pe.wait_ge(wv_hi_done, it + 1)
                    pe.wait_ge(wv_lo_done, it + 1)
                if needed(2 * it - 1 + c):
                    pe.wait_ge(out_added, 2 * it - 1 + c)
                for t in range(CT):
                    bk = (BW0, BW1)[t // 2]
                    toks = slice((c * CT + t) * P, (c * CT + t + 1) * P)
                    for j, (a, b) in enumerate(split3):
                        for k in range(KC):
                            mm = pe.matmul(bk[:, (t % 2) * D:(t % 2 + 1) * D], xT[a][:, k, toks], wv[b][:, k, :],
                                           start=(j == 0 and k == 0), stop=(j == 2 and k == KC - 1))
                mm.then_inc(v_done, 1)

            def project_out(it, c):
                if c == 0:
                    pe.wait_ge(wo_hi_done, it)
                    pe.wait_ge(wo_lo_done, it)
                pe.wait_ge(ao_lo_done, it * 4 - 2 + 2 * c)
                for t in range(CT):
                    bk = (BW0, BW1)[t // 2]
                    for j, (a, b) in enumerate(split3):
                        for h in range(2):
                            mm = pe.matmul(bk[:, (t % 2) * D:(t % 2 + 1) * D], ao[a][c][h][:, t * P:(t + 1) * P], wo[b][:, h, :],
                                           start=(j == 0 and h == 0), stop=(j == 2 and h == 1))
                mm.then_inc(out_done, 1)

            def prepare(g):
                if g == 0:
                    pe.wait_ge(kn_done, 1)
                if g == 2:
                    pe.wait_ge(small_loaded, SMALL_ALL)
                if needed(g):
                    pe.wait_ge(prep_copied, g)
                for m, (_, src, rows, cols) in enumerate(PREP[4 * g:4 * g + 4]):
                    i = pe.transpose(BP[0:rows, m * P:m * P + cols], src, ident[0:cols, 0:cols])
                i.then_inc(prep_ps_done, 1)

            def iteration(it, mode):
                for u in range(4):
                    live = mode != "last"
                    if mode == "first":
                        pe.wait_ge(xT_hi_done, TILES if u else CT)
                        pe.wait_ge(xT_lo_done, TILES if u else CT)
                    if live:
                        project_qk(it, u)
                    if mode == "first":
                        prepare(2 * u)
                    if has(mode, u, 1):
                        scores(it, u)
                    if has(mode, u, 2):
                        transpose_probs(it, u)
                    if u % 2 and live:
                        project_v(it, u // 2)
                    if u % 2 == 0 and mode != "first":
                        if live or u == 0:
                            pe.wait_ge(v_copied, 2 * it + u // 2)
                        else:
                            pe.wait_ge(out_added, 2 * it - 1)
                        project_out(it, u // 2)
                    if has(mode, u, 2):
                        attend(it, u)
                    if mode == "first":
                        prepare(2 * u + 1)

            iteration(0, "first")
            with pe.Fori(1, PAIRS - 1) as it:
                iteration(it, "loop")
            iteration(PAIRS - 1, "end")
            iteration(PAIRS, "last")

            def queries(c):
                pe.wait_ge(xq_done, c + 1)
                for t in range(CT):
                    for k in range(KC):
                        i = pe.transpose(bank[4 + t // 2][:, (t % 2) * D + k * P:(t % 2) * D + (k + 1) * P],
                                         xq_t[c][:, t, k * P:(k + 1) * P], ident)
                i.then_inc(xqT_ps_done, 1)

            def cross_scores(t):
                c = t // CT
                pe.wait_ge(xqT_copied, c + 1)
                if needed(t - 1):
                    pe.wait_ge(xsub_done, t - 1)
                for k in range(KC):
                    bk = bank[2 * (t % 2) + k]
                    pe.matmul(bk[:, :], identb[:, :], xmaskb[:, :].unsqueeze(1).to_broadcast([P, HH, S]),
                              start=True, stop=False, skip_group_check=True)
                    for b in range(2):
                        mm = pe.matmul(bk[b * S:(b + 1) * S, :], qT[c][:, t % CT, k, b * S:(b + 1) * S],
                                       kblk[:, k, 2 * t + b, :, :], start=False, stop=True, skip_group_check=True)
                mm.then_inc(xsc_done, 1)

            pe.wait_ge(out_added, 2 * PAIRS)
            pe.wait_ge(ao_lo_done, 4 * PAIRS)
            queries(0)
            pe.wait_ge(cons_done, 1)
            pe.wait_ge(kblk_loaded, 16 * XH)
            cross_scores(0)
            for t in range(TILES):
                if t == CT - 1:
                    pe.wait_ge(xpT_copied, t)
                    queries(1)
                if t + 1 < TILES:
                    cross_scores(t + 1)
                pe.wait_ge(xprobs_done, t + 1)
                if needed(t):
                    pe.wait_ge(xpT_copied, t)
                if t >= CT - 1:
                    pe.wait_ge(xqT_copied, 2)
                for m in range(HH):
                    i = pe.transpose(bank[4 + m // 4][:, (m % 4) * P:(m % 4 + 1) * P],
                                     xprobs_t[t % 2][:, 2 * m:2 * m + 2, :].rearrange("p h n -> p (h n)"), ident)
                i.then_inc(xpT_ps_done, 1)
                pe.wait_ge(xpT_copied, t + 1)
                if needed(t):
                    pe.wait_ge(xao_copied, t)
                if t == 0:
                    pe.wait_ge(vblk_ready, 2)
                for k in range(KC):
                    for b in range(2):
                        for m in range(4):
                            i = pe.matmul(bank[6][32 * m:32 * m + 32, k * P + b * S:k * P + (b + 1) * S],
                                          vblk[:, 2 * t + b, 2 * k + m // 2, :], xpT_t[0][:, 4 * k + m, b * S:(b + 1) * S],
                                          start=True, stop=True, tile_position=(0, 32 * m))
                i.then_inc(xav_done, 1)
                pe.wait_ge(xao_copied, t + 1)
                if needed(t):
                    pe.wait_ge(x2_done, t)
                for k in range(KC):
                    i = pe.matmul(bank[7][:, 0:D], xaoT_t[t % 2][:, k, :], wxoT[:, k, :], start=(k == 0), stop=(k == KC - 1))
                i.then_inc(xproj_done, 1)

            for c in range(CHUNKS):
                pe.wait_ge(fln_done, c + 1)
                pe.wait_ge(xpT_copied, TILES)
                if needed(c * CT):
                    pe.wait_ge(final_done, c * CT)
                for k in range(KC):
                    for t in range(CT):
                        i = pe.transpose(bank[4 + k][:, t * P:(t + 1) * P], xn[:, c * CT + t, k * P:(k + 1) * P], ident)
                i.then_inc(fT_ps_done, 1)
                pe.wait_ge(fT_copied, c + 1)
                pe.wait_ge(x2_done, TILES)
                if needed(EM * c):
                    pe.wait_ge(fmask_copied, EM * c)
                for t in range(CT):
                    for k in range(KC):
                        i = pe.matmul(bank[7][:, t * E:(t + 1) * E], fT[c][:, k, t * P:(t + 1) * P], wrT[:, k, :], start=(k == 0), stop=(k == KC - 1))
                i.then_inc(logits_done, 1)
                for m in range(EM):
                    if needed(EM * (c - 1) + m + 1):
                        pe.wait_ge(fhm_done, EM * (c - 1) + m + 1)
                    for k in range(KC):
                        i = pe.matmul(bank[m][:, :], aT[:, k, m * P:(m + 1) * P], fT[c][:, k, :], start=(k == 0), stop=(k == KC - 1))
                    i.then_inc(fh_done, 1)
                pe.wait_ge(chosen_done, c + 1)
                for m in range(EM):
                    if needed(EM * c + m - 1):
                        pe.wait_ge(fmask_copied, EM * c + m - 1)
                    for t in range(CT):
                        sel = chosen[:, t * E * R + m * P:t * E * R + (m + 1) * P]
                        i = pe.matmul(bank[6 + m % 2][:, t * P:(t + 1) * P], sel, identb[:, :], start=True, stop=True)
                    i.then_inc(fmask_done, 1)
                pe.wait_ge(fhm_done, EM * (c + 1))
                for t in range(CT):
                    for m in range(EM):
                        i = pe.matmul(bank[4 + t // 2][:, (t % 2) * D:(t % 2 + 1) * D], fhm[:, m, t * P:(t + 1) * P], bT[:, m, :],
                                      start=(m == 0), stop=(m == EM - 1))
                    i.then_inc(y_done, 1)

        @block.vector
        def _(dve):
            steps = [0]

            def step(i):
                steps[0] += 1
                i.then_inc(dve_step, 1)
                dve.wait_ge(dve_step, steps[0])

            def statistics(c, src, ready):
                for t in range(c * CT, (c + 1) * CT):
                    i = dve.bn_stats(bn6[:, t, :], src[:, t, :])
                step(i)
                for t in range(c * CT, (c + 1) * CT):
                    i = dve.bn_aggr(bn2[:, t, :], bn6[:, t, :])
                step(i)
                cs = slice(c * CT, (c + 1) * CT)
                dve.tensor_scalar(veps[:, cs], bn2[:, cs, 1], EPS, None, ALU.add).then_inc(ready, 1)

            def centre(t, src):
                return dve.tensor_scalar(xn[:, t, :], src[:, t, :], bn2[:, t, 0:1], rstd[:, t:t + 1], ALU.subtract, ALU.mult)

            for c in range(CHUNKS):
                dve.wait_ge(x_loaded[c], 16)
                statistics(c, xr, var_done)
            for t in range(TILES):
                dve.wait_ge(rstd_done, t // CT + 1)
                centre(t, xr).then_inc(xn_done, 1)
            for t in range(TILES):
                dve.wait_ge(xT_hi_done, t + 1)
                dve.tensor_tensor(xT_lo[:, :, t * P:(t + 1) * P], bank[2 + t % 2][:, 0:D].rearrange("p (k n) -> p k n", k=KC),
                                  xT_hi[:, :, t * P:(t + 1) * P].bitcast(F32), ALU.subtract).then_inc(xT_lo_done, 1)
            dve.wait_ge(consts_loaded, 16)
            dve.tensor_copy(identb[:, :], ident)
            dve.tensor_copy(xmaskb[:, :], C("xmask")).then_inc(cons_done, 1)
            dve.wait_ge(ctx_loaded, 48)
            dve.wait_ge(rows_loaded, 48)
            ks = masked[0][:, :, :].rearrange("p t n -> p (t n)").rearrange("p (t n) -> p t n", t=TILES)
            kr = masked[1][:, :, :].rearrange("p t n -> p (t n)").rearrange("p (t n) -> p t n", t=TILES)
            step(dve.tensor_tensor(ks, cx[:, :, :], cx[:, :, :], ALU.mult))
            step(dve.tensor_reduce(cssq[:, :], ks, AX_X, ALU.add))
            dve.tensor_scalar(cssq[:, :], cssq[:, :], 1.0 / XC, EPS, ALU.mult, ALU.add).then_inc(cssq_done, 1)
            dve.wait_ge(crr_done, 1)
            step(dve.tensor_tensor(ks, cx[:, :, :], crr[:, :].unsqueeze(2).to_broadcast([P, TILES, XC]), ALU.mult))
            step(dve.tensor_tensor(ks, ks, kw_bc[:, :].unsqueeze(1).to_broadcast([P, TILES, XC]), ALU.mult))
            k4 = ks.rearrange("p t (g f d) -> p (t g) f d", f=2, d=XD // 2)
            r4 = kr.rearrange("p t (g f d) -> p (t g) f d", f=2, d=XD // 2)
            sn = C("xsink").rearrange("p (f d) -> p f d", f=2)
            for f in range(2):
                step(dve.tensor_tensor(r4[:, :, f, :], k4[:, :, 1 - f, :],
                                       sn[:, f, :].unsqueeze(1).to_broadcast([P, TILES * XG, XD // 2]), ALU.mult))
            step(dve.tensor_tensor(ks.rearrange("p t (g d) -> p (t g) d", d=XD), ks.rearrange("p t (g d) -> p (t g) d", d=XD),
                                   C("xcosk").unsqueeze(1).to_broadcast([P, TILES * XG, XD]), ALU.mult))
            dve.tensor_tensor(cx[:, :, :], ks, kr, ALU.add).then_inc(kn_done, 1)
            dve.memset(kblk[:, 1, :, :, :], 0.0).then_inc(kblk_zeroed, 1)

            def rope(it, u):
                n = it * 4 + u
                for i, bk in enumerate((BQ, BK)):
                    cos, sin = C(("cosq", "cosk")[i]), C(("sinq", "sink")[i])
                    dve.wait_ge(qk_swapped[i], n + 1)
                    if needed(n):
                        dve.wait_ge(qk_roped[i], n)
                    dve.tensor_tensor(cos_t[i][:, :].rearrange("p (b n) -> p b n", n=S), bk[:, :].rearrange("p (b n) -> p b n", n=S),
                                      cos.unsqueeze(1).to_broadcast([P, CN // S, S]), ALU.mult).then_inc(qk_cos[i], 1)
                    dve.tensor_tensor(sin_t[i][:, :].rearrange("p (b n) -> p b n", n=S), swapped[i][:, :].rearrange("p (b n) -> p b n", n=S),
                                      sin.unsqueeze(1).to_broadcast([P, CN // S, S]), ALU.mult).then_inc(qk_sin[i], 1)

            def mask_and_max(it, u):
                h, n = (u - 1) % 2, it * 4 + u - 1
                dve.wait_ge(scores_done, n + 1)
                if needed(n - 1):
                    dve.wait_ge(exp_done, n - 1)
                dve.tensor_tensor(masked[h][:, :, :], BS[:, :].rearrange("p (t n) -> p t n", t=CT),
                                  C("mask").unsqueeze(1).to_broadcast([P, CT, P]), ALU.add).then_inc(mask_done, 1)
                dve.wait_ge(mask_done, n + 1)
                dve.tensor_reduce(nmax[h][:, :], masked[h][:, :, :], AX_X, ALU.max, negate=True).then_inc(max_done, 1)

            def reciprocals(it, u):
                h, n = (u - 1) % 2, it * 4 + u - 1
                dve.wait_ge(exp_done, n + 1)
                if needed(n - 1):
                    dve.wait_ge(probs_done, n - 1)
                dve.reciprocal(rrec[h][:, :], rsum[h][:, :]).then_inc(recip_done, 1)

            def add_out(it, c):
                dve.wait_ge(out_done, 2 * it - 1 + c)
                for k, bk in enumerate((BW0, BW1)):
                    ts = slice(c * CT + 2 * k, c * CT + 2 * k + 2)
                    i = dve.tensor_tensor(xr[:, ts, :], bk[:, :].rearrange("p (t n) -> p t n", t=2), xr[:, ts, :], ALU.add)
                i.then_inc(out_added, 1)

            def ao_low(it, u):
                n, c, h = it * 4 + u - 2, ((u - 2) % 4) // 2, u % 2
                dve.wait_ge(ao_hi_done, n + 1)
                dve.tensor_tensor(ao_lo[c][h][:, :], BAV[:, :], ao_hi[c][h][:, :].bitcast(F32), ALU.subtract).then_inc(ao_lo_done, 1)

            def copy_prepared(g):
                dve.wait_ge(prep_ps_done, g + 1)
                for m, (dst, _, rows, cols) in enumerate(PREP[4 * g:4 * g + 4]):
                    i = dve.tensor_copy(dst, BP[0:rows, m * P:m * P + cols])
                i.then_inc(prep_copied, 1)

            def iteration(it, mode):
                for u in range(4):
                    live = mode != "last"
                    if live:
                        rope(it, u)
                    if mode == "first":
                        copy_prepared(2 * u)
                    if has(mode, u, 1):
                        mask_and_max(it, u)
                    if u % 2 == 0 and mode != "first":
                        add_out(it, u // 2)
                    if has(mode, u, 1):
                        reciprocals(it, u)
                    if has(mode, u, 2):
                        ao_low(it, u)
                    if mode == "first":
                        copy_prepared(2 * u + 1)

            iteration(0, "first")
            with dve.Fori(1, PAIRS - 1) as it:
                iteration(it, "loop")
            iteration(PAIRS - 1, "end")
            iteration(PAIRS, "last")

            def residual(t):
                dve.wait_ge(xproj_done, t + 1)
                dve.tensor_tensor(xr[:, t, :], bank[7][:, 0:D], xr[:, t, :], ALU.add).then_inc(x2_done, 1)

            for c in range(CHUNKS):
                cs = slice(c * CT, (c + 1) * CT)
                dve.wait_ge(out_added, 2 * PAIRS - 1 + c)
                statistics(c, xr, xvar_done)
                dve.wait_ge(xrstd_done, c + 1)
                for t in range(c * CT, (c + 1) * CT):
                    i = centre(t, xr)
                i.then_inc(xln_done, 1)
            for c in range(CHUNKS):
                cs = slice(c * CT, (c + 1) * CT)
                dve.wait_ge(xssq_done, c + 1)
                dve.tensor_scalar(ssq[:, cs], ssq[:, cs], 1.0 / D, EPS, ALU.mult, ALU.add).then_inc(xssqe_done, 1)
                dve.wait_ge(xrr_done, c + 1)
                for t in range(c * CT, (c + 1) * CT):
                    i = dve.scalar_tensor_tensor(out=xq_t[c][:, t % CT, :], in0=xn[:, t, :], scalar=rr[:, t:t + 1],
                                                 in1=qw_bc[:, :], op0=ALU.mult, op1=ALU.mult)
                step(i)
                q4 = xq_t[c][:, :, :].rearrange("p t (h f d) -> p (t h) f d", f=2, d=XD // 2)
                o4 = xsin(c).rearrange("p t (h f d) -> p (t h) f d", f=2, d=XD // 2)
                sn = C("xsinq").rearrange("p (f d) -> p f d", f=2)
                dve.tensor_tensor(xcos(c).rearrange("p t (h d) -> p (t h) d", d=XD), xq_t[c][:, :, :].rearrange("p t (h d) -> p (t h) d", d=XD),
                                  C("xcosq").unsqueeze(1).to_broadcast([P, CT * XH, XD]), ALU.mult)
                for f in range(2):
                    i = dve.tensor_tensor(o4[:, :, f, :], q4[:, :, 1 - f, :],
                                          sn[:, f, :].unsqueeze(1).to_broadcast([P, CT * XH, XD // 2]), ALU.mult)
                i.then_inc(xq_sin, 1)
            for t in range(TILES + 1):
                if t < TILES:
                    dve.wait_ge(xsc_done, t + 1)
                    for k in range(KC):
                        i = dve.tensor_reduce(xmx_t[t % 2][:, k * HH:(k + 1) * HH],
                                              bank[2 * (t % 2) + k][:, :].rearrange("p (h n) -> p h n", n=S), AX_X, ALU.max)
                    i.then_inc(xmax_done, 1)
                    dve.wait_ge(xmax_done, t + 1)
                    if needed(t - 1):
                        dve.wait_ge(xprobs_done, t - 1)
                    for k in range(KC):
                        i = dve.tensor_tensor(xsc_t[t % 2][:, k * HH:(k + 1) * HH, :],
                                              bank[2 * (t % 2) + k][:, :].rearrange("p (h n) -> p h n", n=S),
                                              xmx_t[t % 2][:, k * HH:(k + 1) * HH].unsqueeze(2).to_broadcast([P, HH, S]), ALU.subtract)
                    i.then_inc(xsub_done, 1)
                if t >= 2:
                    residual(t - 2)
                if t < TILES:
                    dve.wait_ge(xexp_done, t + 1)
                    step(dve.tensor_reduce(xsm_t[t % 2][:, :], xexp(t), AX_X, ALU.add))
                    dve.reciprocal(xrec(t), xsm_t[t % 2][:, :]).then_inc(xsum_done, 1)
            residual(TILES - 1)

            dve.wait_ge(x2_done, TILES)
            for c in range(CHUNKS):
                statistics(c, xr, fvar_done)
            for c in range(CHUNKS):
                dve.wait_ge(frstd_done, c + 1)
                for t in range(c * CT, (c + 1) * CT):
                    i = centre(t, xr)
                i.then_inc(fln_done, 1)
            for c in range(CHUNKS):
                def row(i, c=c):
                    return lg[:, i, :].rearrange("p (t e) -> p t e", e=E)

                def bc(i):
                    return lgs[:, i, :].unsqueeze(2).to_broadcast([P, CT, E])

                dve.wait_ge(logits_done, c + 1)
                step(dve.tensor_tensor(row(0), bank[7][:, 0:CT * E].rearrange("p (t e) -> p t e", e=E),
                                       br_bc[:, :].unsqueeze(1).to_broadcast([P, CT, E]), ALU.add))
                step(dve.tensor_reduce(lgs[:, 0, :], row(0), AX_X, ALU.max))
                dve.tensor_tensor(row(1), row(0), bc(0), ALU.subtract).then_inc(lshift_done, 1)
                dve.wait_ge(fexp_done, c + 1)
                step(dve.tensor_reduce(lgs[:, 1, :], row(2), AX_X, ALU.add))
                step(dve.reciprocal(lgs[:, 2, :], lgs[:, 1, :]))
                step(dve.tensor_tensor(row(3), row(2), bc(2), ALU.mult))
                step(dve.tensor_reduce(lgs[:, 3, :], row(3), AX_X, ALU.max))
                step(dve.tensor_scalar(wgt[c][:, :], lgs[:, 3, :], 1.0 / R, None, ALU.mult))
                step(dve.tensor_tensor(row(4), row(3), bc(3), ALU.is_equal))
                step(dve.tensor_tensor(row(5), row(4), C("first").unsqueeze(1).to_broadcast([P, CT, E]), ALU.mult))
                step(dve.tensor_reduce(lgs[:, 4, :], row(5), AX_X, ALU.max))
                dve.tensor_tensor(onehot[c][:, :].rearrange("p (t e) -> p t e", e=E), row(5), bc(4), ALU.is_equal).then_inc(onehot_done, 1)
                for m in range(EM):
                    dve.wait_ge(fmask_copied, EM * c + m + 1)
                    dve.wait_ge(fh_done, EM * c + m + 1)
                    if m == 0:
                        if needed(c * CT):
                            dve.wait_ge(y_done, c * CT)
                    dve.tensor_tensor(fhm[:, m, :], bank[m][:, :], fmask[:, m, :], ALU.mult).then_inc(fhm_done, 1)
                for t in range(CT):
                    T = c * CT + t
                    dve.wait_ge(y_done, T + 1)
                    if t % 2 == 0:
                        dve.wait_ge(y_done, T + 2)
                    dve.scalar_tensor_tensor(out=final[:, T, :], in0=bank[4 + t // 2][:, (t % 2) * D:(t % 2 + 1) * D],
                                             scalar=wgt[c][:, t:t + 1], in1=xr[:, T, :], op0=ALU.mult, op1=ALU.add).then_inc(final_done, 1)


_INS = ["x", "ctx_512", "L0_attn_w_qkv", "L0_attn_w_out", "L0_xattn_q_norm_w", "L0_xattn_k_norm_w", "L0_xattn_w_out",
        "L0_ffn_A", "L0_ffn_B", "L0_ffn_Wr", "L0_ffn_br"]


def kernel(**inputs):
    import concourse.bacc as _bacc
    from concourse.bass_utils import run_bass_kernel_spmd as _run

    nc = _bacc.Bacc("TRN2", target_bir_lowering=False, num_devices=1)
    arrays = {f"in_{name}": np.ascontiguousarray(inputs[name]) for name in _INS}
    arrays["in_constants"] = constants()
    args = [nc.dram_tensor(n, a.shape, mybir.dt.from_np(a.dtype), kind="ExternalInput").ap() for n, a in arrays.items()]
    args.append(nc.dram_tensor("out", (B, S, D), F32, kind="ExternalOutput").ap())
    decoder_kernel(nc, *args)
    r = _run(nc, [arrays], core_ids=[0])
    return r.results[0]["out"]
```

```python
from contextlib import ExitStack

import numpy as np

import concourse.bass as bass
from concourse import mybir

ALU = mybir.AluOpType
ACT = mybir.ActivationFunctionType
AX_X = mybir.AxisListType.X
F32 = mybir.dt.float32
F32R = mybir.dt.float32r
BF16 = mybir.dt.bfloat16

P = 128
B, S, D = 16, 64, 256
TILES = B * S // P
KC = D // P
CHUNKS = 2
CT = TILES // CHUNKS
CN = CT * P
HEADS, HD = 16, 128
PAIRS = HEADS // 2
XH, XD = 16, 16
XG = 4
XC = XG * XD
HH = XH // KC
E, R = 8, 64
EM = E * R // P
UNITS = TILES * KC
M_ORDER = (1, 2, 3, 0)
EPS = 1e-5
NEG = -1e30

_COLS = {}
_at = 0
for _name, _n in (("ident", P), ("mask", P), ("xmask", S), ("cosq", S), ("sinq", S), ("cosk", S), ("sink", S),
                  ("xcosq", XD), ("xsinq", XD), ("xcosk", XD), ("xsink", XD), ("first", E)):
    _COLS[_name] = (_at, _at + _n)
    _at += _n
CONST_N = _at


def rope_tables(positions, width):
    inv = (1.0 / 10000.0 ** (np.arange(0, width, 2, dtype=np.float32) / np.float32(width))).astype(np.float32)
    freqs = np.outer(np.arange(positions, dtype=np.float32), inv).astype(np.float32)
    emb = np.concatenate([freqs, freqs], -1)
    sin = np.sin(emb).astype(np.float32)
    sin[:, : width // 2] *= -1.0
    return np.cos(emb).astype(np.float32), sin


def constants():
    c = np.zeros((P, CONST_N), np.float32)

    def put(name, a):
        lo, hi = _COLS[name]
        c[:, lo:hi] = a

    put("ident", np.eye(P))
    p, j = np.arange(P)[:, None], np.arange(P)[None, :]
    put("mask", np.where((p // S == j // S) & (j <= p), 0.0, NEG))
    put("xmask", np.where(np.arange(S)[None, :] <= p % S, 0.0, NEG))
    cos, sin = rope_tables(S, HD)
    scale = np.float32(HD) ** np.float32(-0.5)
    put("cosq", cos.T * scale)
    put("sinq", sin.T * scale)
    put("cosk", cos.T)
    put("sink", sin.T)
    cos, sin = rope_tables(S, XD)
    cos, sin = np.tile(cos, (2, 1)), np.tile(sin, (2, 1))
    scale = np.float32(XD) ** np.float32(-0.5)
    put("xcosq", cos * scale)
    put("xsinq", sin * scale)
    put("xcosk", cos)
    put("xsink", sin)
    put("first", np.arange(E, 0, -1)[None, :])
    return c


def decoder_kernel(nc, x, ctx_in, w_qkv, w_o, q_norm_w, k_norm_w, wx_o, ffn_a, ffn_b, ffn_wr, ffn_br, consts, out):
    x_v = x.rearrange("b s d -> (b s) d").rearrange("(t p) d -> p t d", p=P)
    out_v = out.rearrange("b s d -> (b s) d").rearrange("(t p) d -> p t d", p=P)
    ctx_v = ctx_in.rearrange("b s d -> (b s) d").rearrange("(t p) d -> p t d", p=P)
    wqkv_v = w_qkv.rearrange("(k p) (w n) -> p k w n", p=P, w=3)
    wo_v = w_o.rearrange("(h p) n -> p h n", p=P)

    with ExitStack() as stack:
        def sb(name, shape, dt=F32):
            return stack.enter_context(nc.sbuf_tensor(name, shape, dt))

        def sem(name):
            return stack.enter_context(nc.semaphore(name))

        bank = [stack.enter_context(nc.psum_tensor(f"bank{i}", [P, 512], F32)) for i in range(8)]

        cst = sb("cst", [P, CONST_N])
        identb = sb("identb", [P, P], BF16)
        xmaskb = sb("xmaskb", [P, S], BF16)
        mhalf = sb("mhalf", [P, 16])
        xr = sb("xr", [P, TILES, D])
        xn = sb("xn", [P, TILES, D])
        bn6 = sb("bn6", [P, TILES, 6])
        bn2 = sb("bn2", [P, TILES, 2])
        veps = sb("veps", [P, TILES])
        rstd = sb("rstd", [P, TILES])
        cx = sb("cx", [P, TILES, XC])
        cssq = sb("cssq", [P, TILES])
        crr = sb("crr", [P, TILES])
        kw_bc = sb("kw_bc", [P, XC])
        qw_bc = sb("qw_bc", [P, D])
        kT = sb("kT", [XC, B, S])
        kblk = sb("kblk", [P, KC, B, HH, S])
        vblk = sb("vblk", [P, B, XG, 2 * XD])
        fvar = sb("fvar", [P, TILES])
        qfac = sb("qfac", [P, TILES])
        wxoT = sb("wxoT", [P, KC, D])
        aT = sb("aT", [P, KC, E * R])
        bT = sb("bT", [P, EM, D])
        wrT = sb("wrT", [P, KC, E])
        br_bc = sb("br_bc", [P, E])

        main_mem = ExitStack()

        def sbm(name, shape, dt=F32):
            return main_mem.enter_context(nc.sbuf_tensor(name, shape, dt))

        xT_hi = sbm("xT_hi", [P, KC, TILES * P], F32R)
        xT_lo = sbm("xT_lo", [P, KC, TILES * P], F32R)
        w_st = sbm("w_st", [P, KC, 3, 2 * HD])
        wo_st = sbm("wo_st", [P, 2, D])
        wqk_hi = [sbm(f"wqk_hi{h}", [P, KC, 2, HD], F32R) for h in range(2)]
        wqk_lo = [sbm(f"wqk_lo{h}", [P, KC, 2, HD], F32R) for h in range(2)]
        wv_hi = sbm("wv_hi", [P, KC, 2 * HD], F32R)
        wv_lo = sbm("wv_lo", [P, KC, 2 * HD], F32R)
        wo_hi = sbm("wo_hi", [P, 2, D], F32R)
        wo_lo = sbm("wo_lo", [P, 2, D], F32R)
        swapped = [sbm(f"swapped{i}", [P, CN]) for i in range(2)]
        cos_t = [sbm(f"cos_t{i}", [P, CN]) for i in range(2)]
        sin_t = [sbm(f"sin_t{i}", [P, CN]) for i in range(2)]
        qk = [[sbm(f"qk{h}{i}", [P, CN]) for i in range(2)] for h in range(2)]
        masked = [sbm(f"masked{h}", [P, CT, P]) for h in range(2)]
        nmax = [sbm(f"nmax{h}", [P, CT]) for h in range(2)]
        expd = [sbm(f"expd{h}", [P, CT, P]) for h in range(2)]
        rsum = [sbm(f"rsum{h}", [P, CT]) for h in range(2)]
        rrec = [sbm(f"rrec{h}", [P, CT]) for h in range(2)]
        probs = [sbm(f"probs{h}", [P, CT, P]) for h in range(2)]
        probsT = sbm("probsT", [P, CT, P])
        vals = [sbm(f"vals{c}", [P, CT, 2 * HD]) for c in range(2)]
        with ExitStack() as early:
            cx2 = early.enter_context(nc.sbuf_tensor("cx2", [P, B, XC], F32))
            wst2 = early.enter_context(nc.sbuf_tensor("wst2", [P, KC, D], F32))
            wr_st = early.enter_context(nc.sbuf_tensor("wr_st", [E, D], F32))
        ao_hi = [[sbm(f"ao_hi{c}{h}", [P, CN], F32R) for h in range(2)] for c in range(2)]
        ao_lo = [[sbm(f"ao_lo{c}{h}", [P, CN], F32R) for h in range(2)] for c in range(2)]

        main_mem.close()
        xq = sb("xq", [P, TILES, D])
        xcos_t = [sb(f"xcos{i}", [P, 2, D]) for i in range(2)]

        def duo(d):
            return slice(2 * d, 2 * d + 2)

        def xcos(d):
            return xcos_t[d % 2][:, :, :]

        def xsin(d):
            return xn[:, duo(d), :]
        qT = sb("qT", [P, TILES, KC, P])
        xsc_t = [sb(f"xsc{i}", [P, HH, S]) for i in range(4)]
        xprobs_t = [sb(f"xprobs{i}", [P, HH, S]) for i in range(2)]
        xmx_t = [sb(f"xmx{i}", [P, HH]) for i in range(2)]
        xsm_t = [sb(f"xsm{i}", [P, HH]) for i in range(2)]
        xrec_t = [sb(f"xrec{i}", [P, HH]) for i in range(2)]
        xpT_t = [sb(f"xpT{i}", [P, HH // 2, P]) for i in range(2)]
        xaoT_t = [sb(f"xaoT{i}", [P, KC, P]) for i in range(2)]
        fT = [sb(f"fT{c}", [P, KC, CN]) for c in range(2)]
        fmask_t = [sb(f"fmask{c}", [P, EM, CN], BF16) for c in range(2)]
        fhm_t = [sb(f"fhm{c}", [P, EM, CN]) for c in range(2)]
        lg_t = [sb(f"lg{c}", [P, 6, CT * E]) for c in range(2)]
        lgs_t = [sb(f"lgs{c}", [P, 5, CT]) for c in range(2)]
        onehot = [sb(f"onehot{c}", [P, CT * E], BF16) for c in range(2)]
        chosen = sb("chosen", [P, CT * E * R], BF16)
        wgt = [sb(f"wgt{c}", [P, CT]) for c in range(2)]
        final = sb("final", [P, TILES, D])


        rows_loaded = sem("rows_loaded")
        cssq_done = sem("cssq_done")
        crr_done = sem("crr_done")
        lshift_done = sem("lshift_done")
        consts_loaded = sem("consts_loaded")
        w_loaded = sem("w_loaded")
        wo_loaded = sem("wo_loaded")
        small_loaded = sem("small_loaded")
        ctx_loaded = sem("ctx_loaded")
        kblk_loaded = sem("kblk_loaded")
        out_stored = sem("out_stored")
        dve_step = sem("dve_step")
        pool_step = sem("pool_step")
        var_done = sem("var_done")
        rstd_done = sem("rstd_done")
        xn_done = sem("xn_done")
        xT_ps_done = sem("xT_ps_done")
        xT_hi_done = sem("xT_hi_done")
        xT_lo_done = sem("xT_lo_done")
        wqk_hi_done = sem("wqk_hi_done")
        wqk_lo_done = sem("wqk_lo_done")
        wv_hi_done = sem("wv_hi_done")
        wv_lo_done = sem("wv_lo_done")
        wo_hi_done = sem("wo_hi_done")
        wo_lo_done = sem("wo_lo_done")
        scores_done = sem("scores_done")
        mask_done = sem("mask_done")
        max_done = sem("max_done")
        exp_done = sem("exp_done")
        recip_done = sem("recip_done")
        probs_done = sem("probs_done")
        probsT_ps_done = sem("probsT_ps_done")
        probsT_done = sem("probsT_done")
        v_done = sem("v_done")
        v_copied = sem("v_copied")
        av_done = sem("av_done")
        ao_hi_done = sem("ao_hi_done")
        ao_lo_done = sem("ao_lo_done")
        out_done = sem("out_done")
        out_added = sem("out_added")
        prep_ps_done = sem("prep_ps_done")
        prep_copied = sem("prep_copied")
        cons_done = sem("cons_done")
        kn_done = sem("kn_done")
        kT_ready = sem("kT_ready")
        kblk_zeroed = sem("kblk_zeroed")
        vblk_ready = sem("vblk_ready")
        xvar_done = sem("xvar_done")
        qfac_done = sem("qfac_done")
        xq_sin = sem("xq_sin")
        xq_weighed = sem("xq_weighed")
        xq_done = sem("xq_done")
        xqT_ps_done = sem("xqT_ps_done")
        xqT_copied = sem("xqT_copied")
        xsc_done = sem("xsc_done")
        xmax_done = sem("xmax_done")
        xsub_done = sem("xsub_done")
        xexp_done = sem("xexp_done")
        xsum_done = sem("xsum_done")
        xprobs_done = sem("xprobs_done")
        xpT_ps_done = sem("xpT_ps_done")
        xpT_copied = sem("xpT_copied")
        xav_done = sem("xav_done")
        xao_copied = sem("xao_copied")
        xproj_done = sem("xproj_done")
        x2_done = sem("x2_done")
        fvar_done = sem("fvar_done")
        frstd_done = sem("frstd_done")
        fln_done = sem("fln_done")
        fT_ps_done = sem("fT_ps_done")
        fT_copied = sem("fT_copied")
        logits_done = sem("logits_done")
        fh_done = sem("fh_done")
        fexp_done = sem("fexp_done")
        onehot_done = sem("onehot_done")
        chosen_done = sem("chosen_done")
        fmask_done = sem("fmask_done")
        fmask_copied = sem("fmask_copied")
        fhm_done = sem("fhm_done")
        y_done = sem("y_done")
        final_done = sem("final_done")
        x_loaded = [sem(f"x_loaded{c}") for c in range(CHUNKS)]
        qk_cos = [sem("q_cos"), sem("k_cos")]
        qk_done = [sem("q_done"), sem("k_done")]
        qk_roped = [sem("q_roped"), sem("k_roped")]
        qk_sin = [sem("q_sin"), sem("k_sin")]
        qk_swapped = [sem("q_swapped"), sem("k_swapped")]
        block = stack.enter_context(nc.Block())

        def C(name, rows=slice(0, P)):
            lo, hi = _COLS[name]
            return cst[rows, lo:hi]

        ident = C("ident")
        split3 = [(0, 0), (0, 1), (1, 0)]
        xT = (xT_hi, xT_lo)
        wqk = (wqk_hi, wqk_lo)
        wv = (wv_hi, wv_lo)
        wo = (wo_hi, wo_lo)
        ao = (ao_hi, ao_lo)
        BQ, BK, BS, BT_, BAV, BW0, BW1, BP = bank

        def needed(value):
            return not isinstance(value, int) or value > 0

        def has(mode, u, lag):
            if mode == "first":
                return u - lag >= 0
            if mode == "last":
                return u - lag < 0
            return True

        @block.sync
        def _(sp):
            for c in range(CHUNKS):
                sp.dma_start(xr[:, c * CT:(c + 1) * CT, :], x_v[:, c * CT:(c + 1) * CT, :]).then_inc(x_loaded[c], 16)
            sp.dma_start(cst[:, :], consts).then_inc(consts_loaded, 16)

            def load_w(i):
                for w in range(3):
                    sp.dma_start(w_st[:, :, w, :], wqkv_v[:, :, w, bass.ds(i * 2 * HD, 2 * HD)]).then_inc(w_loaded, 16)

            def load_wo(i):
                sp.dma_start(wo_st[:, :, :], wo_v[:, bass.ds(i * 2, 2), :]).then_inc(wo_loaded, 16)

            load_w(0)
            load_wo(0)
            sp.dma_start(cx[:, :, :], ctx_v).then_inc(ctx_loaded, 16)
            for half in range(2):
                sp.dma_start(cx2[half * S:(half + 1) * S, :, :], ctx_in.rearrange("b s d -> s b d")).then_inc(ctx_loaded, 16)
            small, rows = small_loaded, rows_loaded
            sp.dma_start(kw_bc[:, :], k_norm_w.rearrange("(a n) -> a n", a=1).to_broadcast([P, XC])).then_inc(rows, 16)
            sp.dma_start(qw_bc[:, :], q_norm_w.rearrange("(a n) -> a n", a=1).to_broadcast([P, D])).then_inc(rows, 16)
            sp.dma_start(br_bc[:, :], ffn_br.rearrange("(a n) -> a n", a=1).to_broadcast([P, E])).then_inc(rows, 16)
            sp.dma_start(wr_st[:, :], ffn_wr).then_inc(small, 16)
            sp.dma_start(wst2[:, 0:2, :], wx_o.rearrange("(k p) c -> p k c", p=P)).then_inc(small, 16)
            sp.wait_ge(xT_ps_done, 2 * TILES)
            sp.dma_start(xn[:, 0:4, :], ffn_a.rearrange("e r d -> (e r) d").rearrange("(m p) d -> p m d", p=P)).then_inc(small, 16)
            for k in range(KC):
                sp.dma_start(xn[:, 4 + 2 * k:6 + 2 * k, :].rearrange("p t (e r) -> p (t e) r", r=R),
                             ffn_b[:, k * P:(k + 1) * P, :].rearrange("e o r -> o e r")).then_inc(small, 16)
            with sp.Fori(1, PAIRS) as i:
                sp.wait_ge(wqk_hi_done, i * 2)
                sp.wait_ge(wqk_lo_done, i * 2)
                sp.wait_ge(wv_hi_done, i)
                sp.wait_ge(wv_lo_done, i)
                load_w(i)
                sp.wait_ge(wo_hi_done, i)
                sp.wait_ge(wo_lo_done, i)
                load_wo(i)
            sp.wait_ge(kblk_zeroed, 2)
            sp.wait_ge(prep_copied, 2)
            for h in range(XH):
                k, hh, g = h // HH, h % HH, h // (XH // XG)
                sp.dma_start(kblk[hh * XD:(hh + 1) * XD, k, :, hh, :], kT[g * XD:(g + 1) * XD, :, :]).then_inc(kblk_loaded, 16)
            for t in range(TILES):
                sp.wait_ge(final_done, t + 1)
                sp.dma_start(out_v[:, t, :], final[:, t, :]).then_inc(out_stored, 16)
            sp.wait_ge(out_stored, 16 * TILES)

        @block.gpsimd
        def _(pool):
            pool.memset(mhalf[:, :], -0.5).then_inc(pool_step, 1)
            pool.memset(kblk[:, 0, :, :, :], 0.0).then_inc(kblk_zeroed, 1)
            pool.wait_ge(pool_step, 1)

            for c in range(CHUNKS):
                pool.wait_ge(var_done, c + 1)
                pool.tensor_tensor(rstd[:, c * CT:(c + 1) * CT], veps[:, c * CT:(c + 1) * CT], mhalf[:, 0:CT], ALU.pow).then_inc(rstd_done, 1)

            def lo_qk(h, it):
                pool.wait_ge(wqk_hi_done, it * 2 + h + 1)
                if needed(it):
                    pool.wait_ge(qk_done[1], it * 4 - 1 + h)
                pool.tensor_tensor(wqk_lo[h][:, :, :, :], w_st[:, :, 0:2, h * HD:(h + 1) * HD], wqk_hi[h][:, :, :, :].bitcast(F32), ALU.subtract).then_inc(wqk_lo_done, 1)

            def lo_v(it):
                pool.wait_ge(wv_hi_done, it + 1)
                pool.tensor_tensor(wv_lo[:, :, :], w_st[:, :, 2, :], wv_hi[:, :, :].bitcast(F32), ALU.subtract).then_inc(wv_lo_done, 1)

            def lo_o(it):
                pool.wait_ge(wo_hi_done, it + 1)
                pool.tensor_tensor(wo_lo[:, :, :], wo_st[:, :, :], wo_hi[:, :, :].bitcast(F32), ALU.subtract).then_inc(wo_lo_done, 1)

            lo_qk(0, 0)
            pool.wait_ge(cssq_done, 1)
            pool.tensor_tensor(crr[:, :], cssq[:, :], mhalf[:, 0:TILES], ALU.pow).then_inc(crr_done, 1)
            pool.memset(vblk[:, :, :, :], 0.0).then_inc(pool_step, 1)
            pool.wait_ge(pool_step, 2)
            pool.wait_ge(ctx_loaded, 48)
            for half in range(2):
                rows = slice(half * S, (half + 1) * S)
                pool.tensor_copy(vblk[rows, :, :, half * XD:(half + 1) * XD],
                                 cx2[rows, :, :].rearrange("p b (g d) -> p b g d", g=XG)).then_inc(vblk_ready, 1)
                pool.wait_ge(vblk_ready, half + 1)

            def rope_add(it, u):
                h, n = u % 2, it * 4 + u
                for i in range(2):
                    pool.wait_ge(qk_sin[i], n + 1)
                    if i == 0:
                        if needed(n - 1):
                            pool.wait_ge(scores_done, n - 1)
                    pool.tensor_tensor(qk[h][i][:, :], cos_t[i][:, :], sin_t[i][:, :], ALU.add).then_inc(qk_roped[i], 1)

            def normalise(it, u):
                h, n = (u - 1) % 2, it * 4 + u - 1
                pool.wait_ge(recip_done, n + 1)
                if needed(n - 1):
                    pool.wait_ge(probsT_ps_done, n - 1)
                pool.tensor_tensor(probs[h][:, :, :], expd[h][:, :, :],
                                   rrec[h][:, :].unsqueeze(2).to_broadcast([P, CT, P]), ALU.mult).then_inc(probs_done, 1)

            def iteration(it, mode):
                for u in range(4):
                    if has(mode, u, 0) and mode != "last":
                        if u == 0:
                            lo_qk(1, it)
                            lo_v(it)
                        if u == 3:
                            lo_o(it)
                            if mode != "end":
                                lo_qk(0, it + 1)
                        rope_add(it, u)
                    if has(mode, u, 1):
                        normalise(it, u)

            iteration(0, "first")
            with pool.Fori(1, PAIRS - 1) as it:
                iteration(it, "loop")
            iteration(PAIRS - 1, "end")
            iteration(PAIRS, "last")

            def expert_rstd(d):
                pool.wait_ge(fvar_done, d + 1)
                pool.tensor_tensor(rstd[:, duo(d)], veps[:, duo(d)], mhalf[:, 0:2], ALU.pow).then_inc(frstd_done, 1)

            def rotate_queries(d):
                pool.wait_ge(xvar_done, d + 1)
                pool.tensor_tensor(qfac[:, duo(d)], fvar[:, duo(d)], mhalf[:, 0:2], ALU.pow).then_inc(qfac_done, 1)
                pool.wait_ge(xq_sin, d + 1)
                pool.tensor_tensor(xq[:, duo(d), :], xcos(d), xsin(d), ALU.add).then_inc(xq_done, 1)

            rotate_queries(0)
            rotate_queries(1)
            for v in range(UNITS):
                pool.wait_ge(xsum_done, v + 1)
                if needed(v - 1):
                    pool.wait_ge(xpT_ps_done, v - 1)
                pool.tensor_tensor(xprobs_t[v % 2][:, :, :], xsc_t[v % 4][:, :, :],
                                   xrec_t[v % 2][:, :].unsqueeze(2).to_broadcast([P, HH, S]), ALU.mult).then_inc(xprobs_done, 1)
                if v in (2, 6):
                    rotate_queries(2 + v // 4)
                if v in (7, 11, 15):
                    expert_rstd((v - 7) // 4)
            expert_rstd(3)

        @block.scalar
        def _(act):
            def hi_qk(h, it):
                act.wait_ge(w_loaded, it * 48 + 48)
                if needed(it):
                    act.wait_ge(qk_done[1], it * 4 - 1 + h)
                    act.wait_ge(wqk_lo_done, it * 2 - 1 + h)
                act.activation(wqk_hi[h][:, :, :, :], w_st[:, :, 0:2, h * HD:(h + 1) * HD], ACT.Copy).then_inc(wqk_hi_done, 1)

            def hi_v(it):
                if needed(it):
                    act.wait_ge(v_done, it * 2)
                    act.wait_ge(wv_lo_done, it)
                act.activation(wv_hi[:, :, :], w_st[:, :, 2, :], ACT.Copy).then_inc(wv_hi_done, 1)

            def hi_o(it):
                act.wait_ge(wo_loaded, it * 16 + 16)
                if needed(it):
                    act.wait_ge(out_done, it * 2)
                    act.wait_ge(wo_lo_done, it)
                act.activation(wo_hi[:, :, :], wo_st[:, :, :], ACT.Copy).then_inc(wo_hi_done, 1)

            for t in range(TILES):
                act.wait_ge(xT_ps_done, 2 * t + 2)
                act.activation(xT_hi[:, :, t * P:(t + 1) * P], bank[2 + t % 2][:, 0:D].rearrange("p (k n) -> p k n", k=KC), ACT.Copy).then_inc(xT_hi_done, 1)
                if t == 3:
                    hi_qk(0, 0)

            def swap(it, u):
                n = it * 4 + u
                for i, bk in enumerate((BQ, BK)):
                    act.wait_ge(qk_done[i], n + 1)
                    if needed(n):
                        act.wait_ge(qk_sin[i], n)
                    act.activation(swapped[i][0:S, :], bk[S:P, :], ACT.Copy)
                    act.activation(swapped[i][S:P, :], bk[0:S, :], ACT.Copy).then_inc(qk_swapped[i], 1)

            def exponentials(it, u):
                h, n = (u - 1) % 2, it * 4 + u - 1
                act.wait_ge(max_done, n + 1)
                if needed(n - 1):
                    act.wait_ge(probs_done, n - 1)
                for t in range(CT):
                    i = act.activation(expd[h][:, t, :], masked[h][:, t, :], ACT.Exp, bias=nmax[h][:, t:t + 1],
                                       scale=1.0, accum_out=rsum[h][:, t:t + 1])
                i.then_inc(exp_done, 1)

            def copy_probsT(it, u):
                n = it * 4 + u - 2
                act.wait_ge(probsT_ps_done, n + 1)
                if needed(n):
                    act.wait_ge(av_done, n)
                act.activation(probsT[:, :, :], BT_[:, :].rearrange("p (t n) -> p t n", t=CT), ACT.Copy).then_inc(probsT_done, 1)

            def copy_v(it, c):
                act.wait_ge(v_done, it * 2 + c + 1)
                if needed(it):
                    act.wait_ge(av_done, it * 4 - 2 + 2 * c)
                act.activation(vals[c][:, 0:2, :], BW0[:, :].rearrange("p (t n) -> p t n", t=2), ACT.Copy)
                act.activation(vals[c][:, 2:4, :], BW1[:, :].rearrange("p (t n) -> p t n", t=2), ACT.Copy).then_inc(v_copied, 1)

            def ao_high(it, u):
                n, c, h = it * 4 + u - 2, ((u - 2) % 4) // 2, u % 2
                act.wait_ge(av_done, n + 1)
                act.activation(ao_hi[c][h][:, :], BAV[:, :], ACT.Copy).then_inc(ao_hi_done, 1)

            def iteration(it, mode):
                for u in range(4):
                    live = mode != "last"
                    if live and u == 0:
                        hi_qk(1, it)
                        hi_v(it)
                    if live and u == 3:
                        hi_o(it)
                        if mode != "end":
                            hi_qk(0, it + 1)
                    if live:
                        swap(it, u)
                    if has(mode, u, 2):
                        copy_probsT(it, u)
                    if has(mode, u, 1):
                        exponentials(it, u)
                    if live and u % 2:
                        copy_v(it, u // 2)
                    if has(mode, u, 2):
                        ao_high(it, u)

            iteration(0, "first")
            with act.Fori(1, PAIRS - 1) as it:
                iteration(it, "loop")
            iteration(PAIRS - 1, "end")
            iteration(PAIRS, "last")

            def copy_qT(d):
                act.wait_ge(xqT_ps_done, d + 1)
                act.activation(qT[:, duo(d), :, :], bank[4 + (d == 1)][:, :].rearrange("p (t k n) -> p t k n", t=2, k=KC), ACT.Copy).then_inc(xqT_copied, 1)

            def copy_fT(d):
                act.wait_ge(fT_ps_done, d + 1)
                act.activation(fT[d // 2][:, :, (d % 2) * 2 * P:(d % 2 + 1) * 2 * P],
                               bank[4 + (d == 3)][:, :].rearrange("p (k n) -> p k n", k=KC), ACT.Copy).then_inc(fT_copied, 1)

            copy_qT(0)
            copy_qT(1)
            for v in range(UNITS + 3):
                if v >= 3:
                    w = v - 3
                    act.wait_ge(xav_done, w + 1)
                    if needed(w // 2 - 1):
                        act.wait_ge(xproj_done, w // 2 - 1)
                    act.activation(xaoT_t[w // 2 % 2][:, w % 2, :], bank[6][:, (w % 2) * P:(w % 2 + 1) * P], ACT.Copy).then_inc(xao_copied, 1)
                if 2 <= v < UNITS + 2:
                    w = v - 2
                    act.wait_ge(xpT_ps_done, w + 1)
                    if needed(w - 1):
                        act.wait_ge(xav_done, w - 1)
                    act.activation(xpT_t[w % 2][:, :, :], bank[4 + w % 2][:, :].rearrange("p (m n) -> p m n", m=4), ACT.Copy).then_inc(xpT_copied, 1)
                if v < UNITS:
                    act.wait_ge(xsub_done, v + 1)
                    if v % 4 == 0:
                        act.wait_ge(qfac_done, v // 4 + 1)
                    act.activation(xsc_t[v % 4][:, :, :], xsc_t[v % 4][:, :, :], ACT.Exp, scale=qfac[:, v // 2:v // 2 + 1]).then_inc(xexp_done, 1)
                if v in (5, 9):
                    copy_qT(2 + (v - 5) // 4)
                if v in (11, 15):
                    copy_fT((v - 11) // 4)

            for c in range(CHUNKS):
                act.wait_ge(lshift_done, c + 1)
                act.activation(lg_t[c][:, 2, :], lg_t[c][:, 1, :], ACT.Exp).then_inc(fexp_done, 1)
                if c == 0:
                    copy_fT(2)
                act.wait_ge(onehot_done, c + 1)
                if needed(EM * c):
                    act.wait_ge(fmask_done, EM * c)
                act.activation(chosen[:, :].rearrange("p (n r) -> p n r", r=R), onehot[c][:, :].unsqueeze(2).to_broadcast([P, CT * E, R]), ACT.Copy).then_inc(chosen_done, 1)
                for i, m in enumerate(M_ORDER):
                    act.wait_ge(fmask_done, EM * c + i + 1)
                    act.activation(fmask_t[c][:, m, :], bank[4 + i % 2][:, :], ACT.Copy).then_inc(fmask_copied, 1)
                if c == 0:
                    copy_fT(3)

        def prep_list():
            todo = [(kT[:, :, :].rearrange("p b n -> p (b n)")[:, t * P:(t + 1) * P], cx[:, t, :], XC, P) for t in range(TILES)]
            for k in range(KC):
                for h in range(KC):
                    todo.append((wxoT[:, h, k * P:(k + 1) * P], wst2[:, k, h * P:(h + 1) * P], P, P))
            for k in range(KC):
                todo.append((wrT[:, k, :], wr_st[:, k * P:(k + 1) * P], P, E))
            for m in range(EM):
                for k in range(KC):
                    todo.append((aT[:, k, m * P:(m + 1) * P], xn[:, m, k * P:(k + 1) * P], P, P))
            for k in range(KC):
                for m in range(EM):
                    src = xn[:, 4 + 2 * k:6 + 2 * k, :].rearrange("p t n -> p (t n)")[:, m * P:(m + 1) * P]
                    todo.append((bT[:, m, k * P:(k + 1) * P], src, P, P))
            return todo

        SMALL_ALL = 16 * 5
        PREP = prep_list()

        @block.tensor
        def _(pe):
            pe.wait_ge(consts_loaded, 16)
            for t in range(TILES):
                pe.wait_ge(xn_done, t + 1)
                if needed(t - 1):
                    pe.wait_ge(xT_lo_done, t - 1)
                for k in range(KC):
                    pe.transpose(bank[2 + t % 2][:, k * P:(k + 1) * P], xn[:, t, k * P:(k + 1) * P], ident).then_inc(xT_ps_done, 1)
            def project_qk(it, u):
                c, h, n = u // 2, u % 2, it * 4 + u
                if c == 0:
                    pe.wait_ge(wqk_hi_done, it * 2 + h + 1)
                    pe.wait_ge(wqk_lo_done, it * 2 + h + 1)
                for i, bk in enumerate((BQ, BK)):
                    if needed(n):
                        pe.wait_ge(qk_cos[i], n)
                    for j, (a, b) in enumerate(split3):
                        for k in range(KC):
                            mm = pe.matmul(bk[:, :], wqk[a][h][:, k, i, :], xT[b][:, k, c * CN:(c + 1) * CN],
                                           start=(j == 0 and k == 0), stop=(j == 2 and k == KC - 1))
                    mm.then_inc(qk_done[i], 1)

            def scores(it, u):
                h, n = (u - 1) % 2, it * 4 + u - 1
                pe.wait_ge(qk_roped[1], n + 1)
                if needed(n):
                    pe.wait_ge(mask_done, n)
                for t in range(CT):
                    cols = slice(t * P, (t + 1) * P)
                    mm = pe.matmul(BS[:, cols], qk[h][0][:, cols], qk[h][1][:, cols], start=True, stop=True)
                mm.then_inc(scores_done, 1)

            def transpose_probs(it, u):
                h, n = u % 2, it * 4 + u - 2
                pe.wait_ge(probs_done, n + 1)
                if needed(n):
                    pe.wait_ge(probsT_done, n)
                for t in range(CT):
                    mm = pe.transpose(BT_[:, t * P:(t + 1) * P], probs[h][:, t, :], ident)
                mm.then_inc(probsT_ps_done, 1)

            def attend(it, u):
                h, c, n = u % 2, ((u - 2) % 4) // 2, it * 4 + u - 2
                pe.wait_ge(probsT_done, n + 1)
                pe.wait_ge(v_copied, 2 * it + c + 1 if u >= 2 else 2 * it - 1 + c)
                if needed(n):
                    pe.wait_ge(ao_lo_done, n)
                for t in range(CT):
                    mm = pe.matmul(BAV[:, t * P:(t + 1) * P], vals[c][:, t, h * HD:(h + 1) * HD], probsT[:, t, :], start=True, stop=True)
                mm.then_inc(av_done, 1)

            def project_v(it, c):
                if c == 0:
                    pe.wait_ge(wv_hi_done, it + 1)
                    pe.wait_ge(wv_lo_done, it + 1)
                if needed(2 * it - 1 + c):
                    pe.wait_ge(out_added, 2 * it - 1 + c)
                for t in range(CT):
                    bk = (BW0, BW1)[t // 2]
                    toks = slice((c * CT + t) * P, (c * CT + t + 1) * P)
                    for j, (a, b) in enumerate(split3):
                        for k in range(KC):
                            mm = pe.matmul(bk[:, (t % 2) * D:(t % 2 + 1) * D], xT[a][:, k, toks], wv[b][:, k, :],
                                           start=(j == 0 and k == 0), stop=(j == 2 and k == KC - 1))
                mm.then_inc(v_done, 1)

            def project_out(it, c):
                if c == 0:
                    pe.wait_ge(wo_hi_done, it)
                    pe.wait_ge(wo_lo_done, it)
                pe.wait_ge(ao_lo_done, it * 4 - 2 + 2 * c)
                for t in range(CT):
                    bk = (BW0, BW1)[t // 2]
                    for j, (a, b) in enumerate(split3):
                        for h in range(2):
                            mm = pe.matmul(bk[:, (t % 2) * D:(t % 2 + 1) * D], ao[a][c][h][:, t * P:(t + 1) * P], wo[b][:, h, :],
                                           start=(j == 0 and h == 0), stop=(j == 2 and h == 1))
                mm.then_inc(out_done, 1)

            def prepare(g):
                if g == 0:
                    pe.wait_ge(kn_done, 1)
                if g == 2:
                    pe.wait_ge(small_loaded, SMALL_ALL)
                if needed(g):
                    pe.wait_ge(prep_copied, g)
                for m, (_, src, rows, cols) in enumerate(PREP[4 * g:4 * g + 4]):
                    i = pe.transpose(BP[0:rows, m * P:m * P + cols], src, ident[0:cols, 0:cols])
                i.then_inc(prep_ps_done, 1)

            def iteration(it, mode):
                for u in range(4):
                    live = mode != "last"
                    if mode == "first":
                        pe.wait_ge(xT_hi_done, TILES if u else CT)
                        pe.wait_ge(xT_lo_done, TILES if u else CT)
                    if live:
                        project_qk(it, u)
                    if mode == "first":
                        prepare(2 * u)
                    if has(mode, u, 1):
                        scores(it, u)
                    if has(mode, u, 2):
                        transpose_probs(it, u)
                    if u % 2 and live:
                        project_v(it, u // 2)
                    if u % 2 == 0 and mode != "first":
                        if live or u == 0:
                            pe.wait_ge(v_copied, 2 * it + u // 2)
                        else:
                            pe.wait_ge(out_added, 2 * it - 1)
                        project_out(it, u // 2)
                    if has(mode, u, 2):
                        attend(it, u)
                    if mode == "first":
                        prepare(2 * u + 1)

            iteration(0, "first")
            with pe.Fori(1, PAIRS - 1) as it:
                iteration(it, "loop")
            iteration(PAIRS - 1, "end")
            iteration(PAIRS, "last")

            def queries(d):
                pe.wait_ge(xq_done, d + 1)
                for t in range(2):
                    for k in range(KC):
                        i = pe.transpose(bank[4 + (d == 1)][:, t * D + k * P:t * D + (k + 1) * P], xq[:, 2 * d + t, k * P:(k + 1) * P], ident)
                i.then_inc(xqT_ps_done, 1)

            def tokens(d):
                pe.wait_ge(fln_done, d + 1)
                for k in range(KC):
                    for t in range(2):
                        i = pe.transpose(bank[4 + (d == 3)][:, (2 * k + t) * P:(2 * k + t + 1) * P], xn[:, 2 * d + t, k * P:(k + 1) * P], ident)
                i.then_inc(fT_ps_done, 1)

            def cross_scores(w):
                t, k = w // 2, w % 2
                if w % 4 == 0:
                    pe.wait_ge(xqT_copied, w // 4 + 1)
                if needed(w - 3):
                    pe.wait_ge(xsub_done, w - 3)
                bk = bank[w % 4]
                pe.matmul(bk[:, :], identb[:, :], xmaskb[:, :].unsqueeze(1).to_broadcast([P, HH, S]),
                          start=True, stop=False, skip_group_check=True)
                for b in range(2):
                    mm = pe.matmul(bk[b * S:(b + 1) * S, :], qT[:, t, k, b * S:(b + 1) * S],
                                   kblk[:, k, 2 * t + b, :, :], start=False, stop=True, skip_group_check=True)
                mm.then_inc(xsc_done, 1)

            def cross_project(t):
                pe.wait_ge(xao_copied, 2 * t + 2)
                if needed(t):
                    pe.wait_ge(x2_done, t)
                for k in range(KC):
                    i = pe.matmul(bank[7][:, 0:D], xaoT_t[t % 2][:, k, :], wxoT[:, k, :], start=(k == 0), stop=(k == KC - 1))
                i.then_inc(xproj_done, 1)

            def logits(c):
                pe.wait_ge(fT_copied, 2 * c + 2)
                for t in range(CT):
                    for k in range(KC):
                        i = pe.matmul(bank[0][:, t * E:(t + 1) * E], fT[c][:, k, t * P:(t + 1) * P], wrT[:, k, :], start=(k == 0), stop=(k == KC - 1))
                i.then_inc(logits_done, 1)

            def expand(c, i):
                m = M_ORDER[i]
                if c == 0:
                    pe.wait_ge(xsub_done, UNITS)
                if m == 0:
                    pe.wait_ge(lshift_done, c + 1)
                if needed(EM * (c - 1) + i + 1):
                    pe.wait_ge(fhm_done, EM * (c - 1) + i + 1)
                for k in range(KC):
                    mm = pe.matmul(bank[m][:, :], aT[:, k, m * P:(m + 1) * P], fT[c][:, k, :], start=(k == 0), stop=(k == KC - 1))
                mm.then_inc(fh_done, 1)

            def masks(c):
                pe.wait_ge(chosen_done, c + 1)
                for i, m in enumerate(M_ORDER):
                    if needed(EM * c + i - 1):
                        pe.wait_ge(fmask_copied, EM * c + i - 1)
                    for t in range(CT):
                        sel = chosen[:, t * E * R + m * P:t * E * R + (m + 1) * P]
                        mm = pe.matmul(bank[4 + i % 2][:, t * P:(t + 1) * P], sel, identb[:, :], start=True, stop=True)
                    mm.then_inc(fmask_done, 1)

            def contract(c):
                pe.wait_ge(fhm_done, EM * (c + 1))
                for t in range(CT):
                    bk = bank[(6, 0)[c] + t // 2]
                    for m in range(EM):
                        mm = pe.matmul(bk[:, (t % 2) * D:(t % 2 + 1) * D], fhm_t[c][:, m, t * P:(t + 1) * P], bT[:, m, :],
                                       start=(m == 0), stop=(m == EM - 1))
                    mm.then_inc(y_done, 1)

            pe.wait_ge(ao_lo_done, 4 * PAIRS)
            queries(0)
            pe.wait_ge(out_added, 2 * PAIRS)
            queries(1)
            pe.wait_ge(cons_done, 1)
            pe.wait_ge(kblk_loaded, 16 * XH)
            for w in range(3):
                cross_scores(w)
            pe.wait_ge(vblk_ready, 2)
            for w in range(UNITS):
                pe.wait_ge(xprobs_done, w + 1)
                if w == 0:
                    pe.wait_ge(xqT_copied, 2)
                if needed(w - 1):
                    pe.wait_ge(xpT_copied, w - 1)
                if w in (4, 8):
                    pe.wait_ge(xqT_copied, w // 4 + 2)
                if w in (10, 14):
                    pe.wait_ge(fT_copied, (w - 6) // 4)
                for m in range(HH // 2):
                    i = pe.transpose(bank[4 + w % 2][:, m * P:(m + 1) * P],
                                     xprobs_t[w % 2][:, 2 * m:2 * m + 2, :].rearrange("p h n -> p (h n)"), ident)
                i.then_inc(xpT_ps_done, 1)
                if w + 3 < UNITS:
                    cross_scores(w + 3)
                if w in (3, 7, 9, 13):
                    pe.wait_ge(xpT_copied, w)
                    if w < 8:
                        queries(2 + w // 4)
                    else:
                        tokens((w - 9) // 4)
                if w >= 2 and w % 2 == 0:
                    cross_project(w // 2 - 1)
                if w == UNITS - 2:
                    logits(0)
                if w == UNITS - 1:
                    expand(0, 0)
                t, k = w // 2, w % 2
                pe.wait_ge(xpT_copied, w + 1)
                if needed(w):
                    pe.wait_ge(xao_copied, w)
                for b in range(2):
                    for m in range(4):
                        i = pe.matmul(bank[6][32 * m:32 * m + 32, k * P + b * S:k * P + (b + 1) * S],
                                      vblk[:, 2 * t + b, 2 * k + m // 2, :], xpT_t[w % 2][:, m, b * S:(b + 1) * S],
                                      start=True, stop=True, tile_position=(0, 32 * m))
                i.then_inc(xav_done, 1)

            expand(0, 1)
            cross_project(TILES - 1)
            expand(0, 2)
            expand(0, 3)
            tokens(2)
            pe.wait_ge(fT_copied, 3)
            masks(0)
            pe.wait_ge(fmask_copied, EM)
            tokens(3)
            pe.wait_ge(fhm_done, EM)
            logits(1)
            for i in range(EM):
                expand(1, i)
            masks(1)
            pe.wait_ge(x2_done, TILES)
            contract(0)
            contract(1)

        @block.vector
        def _(dve):
            steps = [0]

            def step(i):
                steps[0] += 1
                i.then_inc(dve_step, 1)
                dve.wait_ge(dve_step, steps[0])

            def statistics(c, src, ready):
                for t in range(c * CT, (c + 1) * CT):
                    i = dve.bn_stats(bn6[:, t, :], src[:, t, :])
                step(i)
                for t in range(c * CT, (c + 1) * CT):
                    i = dve.bn_aggr(bn2[:, t, :], bn6[:, t, :])
                step(i)
                cs = slice(c * CT, (c + 1) * CT)
                dve.tensor_scalar(veps[:, cs], bn2[:, cs, 1], EPS, None, ALU.add).then_inc(ready, 1)

            def centre(t, src):
                return dve.tensor_scalar(xn[:, t, :], src[:, t, :], bn2[:, t, 0:1], rstd[:, t:t + 1], ALU.subtract, ALU.mult)

            for c in range(CHUNKS):
                dve.wait_ge(x_loaded[c], 16)
                statistics(c, xr, var_done)
            for t in range(TILES):
                dve.wait_ge(rstd_done, t // CT + 1)
                centre(t, xr).then_inc(xn_done, 1)
            for t in range(TILES):
                dve.wait_ge(xT_hi_done, t + 1)
                dve.tensor_tensor(xT_lo[:, :, t * P:(t + 1) * P], bank[2 + t % 2][:, 0:D].rearrange("p (k n) -> p k n", k=KC),
                                  xT_hi[:, :, t * P:(t + 1) * P].bitcast(F32), ALU.subtract).then_inc(xT_lo_done, 1)
            dve.wait_ge(consts_loaded, 16)
            dve.tensor_copy(identb[:, :], ident)
            dve.tensor_copy(xmaskb[:, :], C("xmask")).then_inc(cons_done, 1)
            dve.wait_ge(ctx_loaded, 48)
            dve.wait_ge(rows_loaded, 48)
            ks = masked[0][:, :, :].rearrange("p t n -> p (t n)").rearrange("p (t n) -> p t n", t=TILES)
            kr = masked[1][:, :, :].rearrange("p t n -> p (t n)").rearrange("p (t n) -> p t n", t=TILES)
            step(dve.tensor_tensor(ks, cx[:, :, :], cx[:, :, :], ALU.mult))
            step(dve.tensor_reduce(cssq[:, :], ks, AX_X, ALU.add))
            dve.tensor_scalar(cssq[:, :], cssq[:, :], 1.0 / XC, EPS, ALU.mult, ALU.add).then_inc(cssq_done, 1)
            dve.wait_ge(crr_done, 1)
            step(dve.tensor_tensor(ks, cx[:, :, :], crr[:, :].unsqueeze(2).to_broadcast([P, TILES, XC]), ALU.mult))
            step(dve.tensor_tensor(ks, ks, kw_bc[:, :].unsqueeze(1).to_broadcast([P, TILES, XC]), ALU.mult))
            k4 = ks.rearrange("p t (g f d) -> p (t g) f d", f=2, d=XD // 2)
            r4 = kr.rearrange("p t (g f d) -> p (t g) f d", f=2, d=XD // 2)
            sn = C("xsink").rearrange("p (f d) -> p f d", f=2)
            for f in range(2):
                step(dve.tensor_tensor(r4[:, :, f, :], k4[:, :, 1 - f, :],
                                       sn[:, f, :].unsqueeze(1).to_broadcast([P, TILES * XG, XD // 2]), ALU.mult))
            step(dve.tensor_tensor(ks.rearrange("p t (g d) -> p (t g) d", d=XD), ks.rearrange("p t (g d) -> p (t g) d", d=XD),
                                   C("xcosk").unsqueeze(1).to_broadcast([P, TILES * XG, XD]), ALU.mult))
            dve.tensor_tensor(cx[:, :, :], ks, kr, ALU.add).then_inc(kn_done, 1)
            dve.memset(kblk[:, 1, :, :, :], 0.0).then_inc(kblk_zeroed, 1)

            def rope(it, u):
                n = it * 4 + u
                for i, bk in enumerate((BQ, BK)):
                    cos, sin = C(("cosq", "cosk")[i]), C(("sinq", "sink")[i])
                    dve.wait_ge(qk_swapped[i], n + 1)
                    if needed(n):
                        dve.wait_ge(qk_roped[i], n)
                    dve.tensor_tensor(cos_t[i][:, :].rearrange("p (b n) -> p b n", n=S), bk[:, :].rearrange("p (b n) -> p b n", n=S),
                                      cos.unsqueeze(1).to_broadcast([P, CN // S, S]), ALU.mult).then_inc(qk_cos[i], 1)
                    dve.tensor_tensor(sin_t[i][:, :].rearrange("p (b n) -> p b n", n=S), swapped[i][:, :].rearrange("p (b n) -> p b n", n=S),
                                      sin.unsqueeze(1).to_broadcast([P, CN // S, S]), ALU.mult).then_inc(qk_sin[i], 1)

            def mask_and_max(it, u):
                h, n = (u - 1) % 2, it * 4 + u - 1
                dve.wait_ge(scores_done, n + 1)
                if needed(n - 1):
                    dve.wait_ge(exp_done, n - 1)
                dve.tensor_tensor(masked[h][:, :, :], BS[:, :].rearrange("p (t n) -> p t n", t=CT),
                                  C("mask").unsqueeze(1).to_broadcast([P, CT, P]), ALU.add).then_inc(mask_done, 1)
                dve.wait_ge(mask_done, n + 1)
                dve.tensor_reduce(nmax[h][:, :], masked[h][:, :, :], AX_X, ALU.max, negate=True).then_inc(max_done, 1)

            def reciprocals(it, u):
                h, n = (u - 1) % 2, it * 4 + u - 1
                dve.wait_ge(exp_done, n + 1)
                if needed(n - 1):
                    dve.wait_ge(probs_done, n - 1)
                dve.reciprocal(rrec[h][:, :], rsum[h][:, :]).then_inc(recip_done, 1)

            def add_out(it, c):
                dve.wait_ge(out_done, 2 * it - 1 + c)
                for k, bk in enumerate((BW0, BW1)):
                    ts = slice(c * CT + 2 * k, c * CT + 2 * k + 2)
                    i = dve.tensor_tensor(xr[:, ts, :], bk[:, :].rearrange("p (t n) -> p t n", t=2), xr[:, ts, :], ALU.add)
                i.then_inc(out_added, 1)

            def ao_low(it, u):
                n, c, h = it * 4 + u - 2, ((u - 2) % 4) // 2, u % 2
                dve.wait_ge(ao_hi_done, n + 1)
                dve.tensor_tensor(ao_lo[c][h][:, :], BAV[:, :], ao_hi[c][h][:, :].bitcast(F32), ALU.subtract).then_inc(ao_lo_done, 1)

            def copy_prepared(g):
                dve.wait_ge(prep_ps_done, g + 1)
                for m, (dst, _, rows, cols) in enumerate(PREP[4 * g:4 * g + 4]):
                    i = dve.tensor_copy(dst, BP[0:rows, m * P:m * P + cols])
                i.then_inc(prep_copied, 1)

            def iteration(it, mode):
                for u in range(4):
                    live = mode != "last"
                    if live:
                        rope(it, u)
                    if mode == "first":
                        copy_prepared(2 * u)
                    if has(mode, u, 1):
                        mask_and_max(it, u)
                    if u % 2 == 0 and mode != "first":
                        add_out(it, u // 2)
                    if has(mode, u, 1):
                        reciprocals(it, u)
                    if has(mode, u, 2):
                        ao_low(it, u)
                    if mode == "first":
                        copy_prepared(2 * u + 1)
                    if mode == "last" and u in (1, 2):
                        for part in range(4):
                            query_part(u - 1, part)

            def query_part(d, part):
                x3 = "p t (h d) -> p (t h) d"
                x4 = "p t (h f d) -> p (t h) f d"
                if part == 0:
                    dve.wait_ge(out_added, 2 * PAIRS - 1 + d // 2)
                    for t in range(2 * d, 2 * d + 2):
                        i = dve.bn_stats(bn6[:, t, :], xr[:, t, :])
                    step(i)
                    for t in range(2 * d, 2 * d + 2):
                        i = dve.bn_aggr(bn2[:, t, :], bn6[:, t, :])
                    step(i)
                    dve.tensor_scalar(fvar[:, duo(d)], bn2[:, duo(d), 1], 1.0 + EPS, EPS * EPS, ALU.mult, ALU.add).then_inc(xvar_done, 1)
                if part == 1:
                    for t in range(2 * d, 2 * d + 2):
                        i = dve.scalar_tensor_tensor(out=xq[:, t, :], in0=xr[:, t, :], scalar=bn2[:, t, 0:1],
                                                     in1=qw_bc[:, :], op0=ALU.subtract, op1=ALU.mult)
                    i.then_inc(xq_weighed, 1)
                if part == 2:
                    dve.wait_ge(xq_weighed, d + 1)
                    if needed(d - 1):
                        dve.wait_ge(xq_done, d - 1)
                    dve.tensor_tensor(xcos(d).rearrange(x3, d=XD), xq[:, duo(d), :].rearrange(x3, d=XD),
                                      C("xcosq").unsqueeze(1).to_broadcast([P, 2 * XH, XD]), ALU.mult)
                if part == 3:
                    q4, o4 = xq[:, duo(d), :].rearrange(x4, f=2, d=XD // 2), xsin(d).rearrange(x4, f=2, d=XD // 2)
                    sn = C("xsinq").rearrange("p (f d) -> p f d", f=2)
                    for f in range(2):
                        i = dve.tensor_tensor(o4[:, :, f, :], q4[:, :, 1 - f, :],
                                              sn[:, f, :].unsqueeze(1).to_broadcast([P, 2 * XH, XD // 2]), ALU.mult)
                    i.then_inc(xq_sin, 1)

            def expert_stats(d):
                dve.wait_ge(x2_done, 2 * d + 2)
                for t in range(2 * d, 2 * d + 2):
                    i = dve.bn_stats(bn6[:, t, :], xr[:, t, :])
                step(i)
                for t in range(2 * d, 2 * d + 2):
                    i = dve.bn_aggr(bn2[:, t, :], bn6[:, t, :])
                step(i)
                dve.tensor_scalar(veps[:, duo(d)], bn2[:, duo(d), 1], EPS, None, ALU.add).then_inc(fvar_done, 1)

            def expert_centre(d):
                dve.wait_ge(frstd_done, d + 1)
                for t in range(2 * d, 2 * d + 2):
                    i = centre(t, xr)
                i.then_inc(fln_done, 1)

            iteration(0, "first")
            with dve.Fori(1, PAIRS - 1) as it:
                iteration(it, "loop")
            iteration(PAIRS - 1, "end")
            iteration(PAIRS, "last")

            def residual(t):
                dve.wait_ge(xproj_done, t + 1)
                dve.tensor_tensor(xr[:, t, :], bank[7][:, 0:D], xr[:, t, :], ALU.add).then_inc(x2_done, 1)

            for v in range(UNITS + 1):
                if v < UNITS:
                    dve.wait_ge(xsc_done, v + 1)
                    dve.tensor_reduce(xmx_t[v % 2][:, :], bank[v % 4][:, :].rearrange("p (h n) -> p h n", n=S), AX_X, ALU.max).then_inc(xmax_done, 1)
                if v >= 1:
                    dve.wait_ge(xexp_done, v)
                    if needed(v - 2):
                        dve.wait_ge(xprobs_done, v - 2)
                    step(dve.tensor_reduce(xsm_t[(v - 1) % 2][:, :], xsc_t[(v - 1) % 4][:, :, :], AX_X, ALU.add))
                    dve.reciprocal(xrec_t[(v - 1) % 2][:, :], xsm_t[(v - 1) % 2][:, :]).then_inc(xsum_done, 1)
                if v < UNITS:
                    dve.wait_ge(xmax_done, v + 1)
                    if needed(v - 3):
                        dve.wait_ge(xprobs_done, v - 3)
                    dve.tensor_tensor(xsc_t[v % 4][:, :, :], bank[v % 4][:, :].rearrange("p (h n) -> p h n", n=S),
                                      xmx_t[v % 2][:, :].unsqueeze(2).to_broadcast([P, HH, S]), ALU.subtract).then_inc(xsub_done, 1)
                if v < 8:
                    query_part(2 + v // 4, v % 4)
                if v >= 5 and v % 2:
                    residual((v - 5) // 2)
                if v in (7, 11, 15):
                    expert_stats((v - 7) // 4)
                if v in (9, 13):
                    expert_centre((v - 9) // 4)

            def gate_shift(c):
                lg, lgs = lg_t[c], lgs_t[c]
                dve.wait_ge(logits_done, c + 1)
                step(dve.tensor_tensor(lg[:, 0, :].rearrange("p (t e) -> p t e", e=E), bank[0][:, 0:CT * E].rearrange("p (t e) -> p t e", e=E),
                                       br_bc[:, :].unsqueeze(1).to_broadcast([P, CT, E]), ALU.add))
                step(dve.tensor_reduce(lgs[:, 0, :], lg[:, 0, :].rearrange("p (t e) -> p t e", e=E), AX_X, ALU.max))
                dve.tensor_tensor(lg[:, 1, :].rearrange("p (t e) -> p t e", e=E), lg[:, 0, :].rearrange("p (t e) -> p t e", e=E),
                                  lgs[:, 0, :].unsqueeze(2).to_broadcast([P, CT, E]), ALU.subtract).then_inc(lshift_done, 1)

            def choose(c):
                lg, lgs = lg_t[c], lgs_t[c]

                def row(i):
                    return lg[:, i, :].rearrange("p (t e) -> p t e", e=E)

                def bc(i):
                    return lgs[:, i, :].unsqueeze(2).to_broadcast([P, CT, E])

                dve.wait_ge(fexp_done, c + 1)
                step(dve.tensor_reduce(lgs[:, 1, :], row(2), AX_X, ALU.add))
                step(dve.reciprocal(lgs[:, 2, :], lgs[:, 1, :]))
                step(dve.tensor_tensor(row(3), row(2), bc(2), ALU.mult))
                step(dve.tensor_reduce(lgs[:, 3, :], row(3), AX_X, ALU.max))
                step(dve.tensor_scalar(wgt[c][:, :], lgs[:, 3, :], 1.0 / R, None, ALU.mult))
                step(dve.tensor_tensor(row(4), row(3), bc(3), ALU.is_equal))
                step(dve.tensor_tensor(row(5), row(4), C("first").unsqueeze(1).to_broadcast([P, CT, E]), ALU.mult))
                step(dve.tensor_reduce(lgs[:, 4, :], row(5), AX_X, ALU.max))
                dve.tensor_tensor(onehot[c][:, :].rearrange("p (t e) -> p t e", e=E), row(5), bc(4), ALU.is_equal).then_inc(onehot_done, 1)

            def mask_inner(c):
                for i, m in enumerate(M_ORDER):
                    dve.wait_ge(fmask_copied, EM * c + i + 1)
                    dve.wait_ge(fh_done, EM * c + i + 1)
                    dve.tensor_tensor(fhm_t[c][:, m, :], bank[m][:, :], fmask_t[c][:, m, :], ALU.mult).then_inc(fhm_done, 1)

            residual(TILES - 2)
            expert_centre(2)
            gate_shift(0)
            residual(TILES - 1)
            choose(0)
            expert_stats(3)
            expert_centre(3)
            mask_inner(0)
            gate_shift(1)
            choose(1)
            mask_inner(1)
            for t in range(TILES):
                if t % 2 == 0:
                    dve.wait_ge(y_done, t + 2)
                dve.scalar_tensor_tensor(out=final[:, t, :], in0=bank[(6, 0)[t // CT] + t % CT // 2][:, (t % 2) * D:(t % 2 + 1) * D],
                                         scalar=wgt[t // CT][:, t % CT:t % CT + 1], in1=xr[:, t, :], op0=ALU.mult, op1=ALU.add).then_inc(final_done, 1)


_INS = ["x", "ctx_512", "L0_attn_w_qkv", "L0_attn_w_out", "L0_xattn_q_norm_w", "L0_xattn_k_norm_w", "L0_xattn_w_out",
        "L0_ffn_A", "L0_ffn_B", "L0_ffn_Wr", "L0_ffn_br"]


def kernel(**inputs):
    import concourse.bacc as _bacc
    from concourse.bass_utils import run_bass_kernel_spmd as _run

    nc = _bacc.Bacc("TRN2", target_bir_lowering=False, num_devices=1)
    arrays = {f"in_{name}": np.ascontiguousarray(inputs[name]) for name in _INS}
    arrays["in_constants"] = constants()
    args = [nc.dram_tensor(n, a.shape, mybir.dt.from_np(a.dtype), kind="ExternalInput").ap() for n, a in arrays.items()]
    args.append(nc.dram_tensor("out", (B, S, D), F32, kind="ExternalOutput").ap())
    decoder_kernel(nc, *args)
    r = _run(nc, [arrays], core_ids=[0])
    return r.results[0]["out"]
```

```python
from contextlib import ExitStack

import numpy as np

import concourse.bass as bass
from concourse import mybir

ALU = mybir.AluOpType
ACT = mybir.ActivationFunctionType
AX_X = mybir.AxisListType.X
F32 = mybir.dt.float32
F32R = mybir.dt.float32r
BF16 = mybir.dt.bfloat16

P = 128
B, S, D = 16, 64, 256
TILES = B * S // P
KC = D // P
CHUNKS = 2
CT = TILES // CHUNKS
CN = CT * P
HEADS, HD = 16, 128
PAIRS = HEADS // 2
XH, XD = 16, 16
XG = 4
XC = XG * XD
HH = XH // KC
E, R = 8, 64
EM = E * R // P
UNITS = TILES * KC
M_ORDER = (1, 2, 3, 0)
MASK_BANKS = (4, 5, 7, 4)
XT_BANKS = (2, 5, 3, 4)
EPS = 1e-5
NEG = -1e30

_COLS = {}
_at = 0
for _name, _n in (("ident", P), ("mask", P), ("xmask", S), ("cosq", S), ("sinq", S), ("cosk", S), ("sink", S),
                  ("xcosq", XD), ("xsinq", XD), ("xcosk", XD), ("xsink", XD), ("first", E)):
    _COLS[_name] = (_at, _at + _n)
    _at += _n
CONST_N = _at


def rope_tables(positions, width):
    inv = (1.0 / 10000.0 ** (np.arange(0, width, 2, dtype=np.float32) / np.float32(width))).astype(np.float32)
    freqs = np.outer(np.arange(positions, dtype=np.float32), inv).astype(np.float32)
    emb = np.concatenate([freqs, freqs], -1)
    sin = np.sin(emb).astype(np.float32)
    sin[:, : width // 2] *= -1.0
    return np.cos(emb).astype(np.float32), sin


def constants():
    c = np.zeros((P, CONST_N), np.float32)

    def put(name, a):
        lo, hi = _COLS[name]
        c[:, lo:hi] = a

    put("ident", np.eye(P))
    p, j = np.arange(P)[:, None], np.arange(P)[None, :]
    put("mask", np.where((p // S == j // S) & (j <= p), 0.0, NEG))
    put("xmask", np.where(np.arange(S)[None, :] <= p % S, 0.0, NEG))
    cos, sin = rope_tables(S, HD)
    scale = np.float32(HD) ** np.float32(-0.5)
    put("cosq", cos.T * scale)
    put("sinq", sin.T * scale)
    put("cosk", cos.T)
    put("sink", sin.T)
    cos, sin = rope_tables(S, XD)
    cos, sin = np.tile(cos, (2, 1)), np.tile(sin, (2, 1))
    scale = np.float32(XD) ** np.float32(-0.5)
    put("xcosq", cos * scale)
    put("xsinq", sin * scale)
    put("xcosk", cos)
    put("xsink", sin)
    put("first", np.arange(E, 0, -1)[None, :])
    return c


def decoder_kernel(nc, x, ctx_in, w_qkv, w_o, q_norm_w, k_norm_w, wx_o, ffn_a, ffn_b, ffn_wr, ffn_br, consts, out):
    x_v = x.rearrange("b s d -> (b s) d").rearrange("(t p) d -> p t d", p=P)
    out_v = out.rearrange("b s d -> (b s) d").rearrange("(t p) d -> p t d", p=P)
    ctx_v = ctx_in.rearrange("b s d -> (b s) d").rearrange("(t p) d -> p t d", p=P)
    wqkv_v = w_qkv.rearrange("(k p) (w n) -> p k w n", p=P, w=3)
    wo_v = w_o.rearrange("(h p) n -> p h n", p=P)

    with ExitStack() as stack:
        def sb(name, shape, dt=F32):
            return stack.enter_context(nc.sbuf_tensor(name, shape, dt))

        def sem(name):
            return stack.enter_context(nc.semaphore(name))

        bank = [stack.enter_context(nc.psum_tensor(f"bank{i}", [P, 512], F32)) for i in range(8)]

        cst = sb("cst", [P, CONST_N])
        identb = sb("identb", [P, P], BF16)
        xmaskb = sb("xmaskb", [P, S], BF16)
        mhalf = sb("mhalf", [P, 16])
        xr = sb("xr", [P, TILES, D])
        xn = sb("xn", [P, TILES, D])
        bn6 = sb("bn6", [P, TILES, 6])
        bn2 = sb("bn2", [P, TILES, 2])
        veps = sb("veps", [P, TILES])
        rstd = sb("rstd", [P, TILES])
        cx = sb("cx", [P, TILES, XC])
        cssq = sb("cssq", [P, TILES])
        crr = sb("crr", [P, TILES])
        kw_bc = sb("kw_bc", [P, XC])
        qw_bc = sb("qw_bc", [P, D])
        kT = sb("kT", [XC, B, S])
        kblk = sb("kblk", [P, KC, B, HH, S])
        vblk = sb("vblk", [P, B, XG, 2 * XD])
        fvar = sb("fvar", [P, TILES])
        qfac = sb("qfac", [P, TILES])
        xmx_t = [sb(f"xmx{i}", [P, HH]) for i in range(2)]
        xsm_t = [sb(f"xsm{i}", [P, HH]) for i in range(2)]
        xrec_t = [sb(f"xrec{i}", [P, HH]) for i in range(2)]
        wxoT = sb("wxoT", [P, KC, D])
        aT = sb("aT", [P, KC, E * R])
        bT = sb("bT", [P, EM, D])
        wrT = sb("wrT", [P, KC, E])
        br_bc = sb("br_bc", [P, E])

        main_mem = ExitStack()

        def sbm(name, shape, dt=F32):
            return main_mem.enter_context(nc.sbuf_tensor(name, shape, dt))

        xT_hi = sbm("xT_hi", [P, KC, TILES * P], F32R)
        xT_lo = sbm("xT_lo", [P, KC, TILES * P], F32R)
        w_st = sbm("w_st", [P, KC, 3, 2 * HD])
        wo_st = sbm("wo_st", [P, 2, D])
        wqk_hi = [sbm(f"wqk_hi{h}", [P, KC, 2, HD], F32R) for h in range(2)]
        wqk_lo = [sbm(f"wqk_lo{h}", [P, KC, 2, HD], F32R) for h in range(2)]
        wv_hi = sbm("wv_hi", [P, KC, 2 * HD], F32R)
        wv_lo = sbm("wv_lo", [P, KC, 2 * HD], F32R)
        wo_hi = sbm("wo_hi", [P, 2, D], F32R)
        wo_lo = sbm("wo_lo", [P, 2, D], F32R)
        swapped = [sbm(f"swapped{i}", [P, CN]) for i in range(2)]
        cos_t = [sbm(f"cos_t{i}", [P, CN]) for i in range(2)]
        sin_t = [sbm(f"sin_t{i}", [P, CN]) for i in range(2)]
        qk = [[sbm(f"qk{h}{i}", [P, CN]) for i in range(2)] for h in range(2)]
        masked = [sbm(f"masked{h}", [P, CT, P]) for h in range(2)]
        nmax = [sbm(f"nmax{h}", [P, CT]) for h in range(2)]
        expd = [sbm(f"expd{h}", [P, CT, P]) for h in range(2)]
        rsum = [sbm(f"rsum{h}", [P, CT]) for h in range(2)]
        rrec = [sbm(f"rrec{h}", [P, CT]) for h in range(2)]
        probs = [sbm(f"probs{h}", [P, CT, P]) for h in range(2)]
        probsT = sbm("probsT", [P, CT, P])
        vals = [sbm(f"vals{c}", [P, CT, 2 * HD]) for c in range(2)]
        with ExitStack() as early:
            cx2 = early.enter_context(nc.sbuf_tensor("cx2", [P, B, XC], F32))
            ks = early.enter_context(nc.sbuf_tensor("ks", [P, TILES, XC], F32))
            kr = early.enter_context(nc.sbuf_tensor("kr", [P, TILES, XC], F32))
            wst2 = early.enter_context(nc.sbuf_tensor("wst2", [P, KC, D], F32))
            wr_st = early.enter_context(nc.sbuf_tensor("wr_st", [E, D], F32))
        ao_hi, ao_lo = [[], []], [[], []]
        for c in (1, 0):
            ao_hi[c] = [sbm(f"ao_hi{c}{h}", [P, CN], F32R) for h in range(2)]
            ao_lo[c] = [sbm(f"ao_lo{c}{h}", [P, CN], F32R) for h in range(2)]

        main_mem.close()
        with ExitStack() as query_mem:
            xq = query_mem.enter_context(nc.sbuf_tensor("xq", [P, TILES, D], F32))
            xcos_t = [query_mem.enter_context(nc.sbuf_tensor(f"xcos{i}", [P, 2, D], F32)) for i in range(2)]
            qT = query_mem.enter_context(nc.sbuf_tensor("qT", [P, TILES, KC, P], F32))
        fhm_lo = [sb(f"fhm_lo{c}", [P, EM, CN], F32R) for c in range(2)]
        chosen = sb("chosen", [P, CT * E * R], BF16)

        def duo(d):
            return slice(2 * d, 2 * d + 2)

        def xcos(d):
            return xcos_t[d % 2][:, :, :]

        def xsin(d):
            return xn[:, duo(d), :]
        with ExitStack() as unit_mem:
            xsc_t = [unit_mem.enter_context(nc.sbuf_tensor(f"xsc{i}", [P, HH, S], F32)) for i in range(4)]
            xprobs_t = [unit_mem.enter_context(nc.sbuf_tensor(f"xprobs{i}", [P, HH, S], F32)) for i in range(2)]
            xpT_t = [unit_mem.enter_context(nc.sbuf_tensor(f"xpT{i}", [P, HH // 2, P], F32)) for i in range(2)]
        fhm_hi = [sb(f"fhm_hi{c}", [P, EM, CN], F32R) for c in range(2)]
        xaoT_t = [sb(f"xaoT{i}", [P, KC, P]) for i in range(2)]
        fT = [sb(f"fT{c}", [P, KC, CN]) for c in range(2)]
        fmask = sb("fmask", [P, EM, CN], BF16)
        fT_hi = [sb(f"fT_hi{c}", [P, KC, CN], F32R) for c in range(2)]
        fT_lo = [sb(f"fT_lo{c}", [P, KC, CN], F32R) for c in range(2)]
        aT_hi = sb("aT_hi", [P, KC, E * R], F32R)
        aT_lo = sb("aT_lo", [P, KC, E * R], F32R)
        bT_lo = sb("bT_lo", [P, EM, D], F32R)
        bT_hi = sb("bT_hi", [P, EM, D], F32R)
        fhm = sb("fhm", [P, EM, CN])
        lg_t = [sb(f"lg{c}", [P, 6, CT * E]) for c in range(2)]
        lgs_t = [sb(f"lgs{c}", [P, 5, CT]) for c in range(2)]
        onehot = [sb(f"onehot{c}", [P, CT * E], BF16) for c in range(2)]
        wgt = [sb(f"wgt{c}", [P, CT]) for c in range(2)]
        final = xn


        rows_loaded = sem("rows_loaded")
        cssq_done = sem("cssq_done")
        crr_done = sem("crr_done")
        lshift_done = sem("lshift_done")
        consts_loaded = sem("consts_loaded")
        ident_loaded = sem("ident_loaded")
        wqk_loaded = sem("wqk_loaded")
        wv_loaded = sem("wv_loaded")
        wo_loaded = sem("wo_loaded")
        small_loaded = sem("small_loaded")
        ab_loaded = sem("ab_loaded")
        vblk_zeroed = sem("vblk_zeroed")
        ctx_loaded = sem("ctx_loaded")
        kblk_loaded = sem("kblk_loaded")
        out_stored = sem("out_stored")
        dve_step = sem("dve_step")
        pool_step = sem("pool_step")
        var_done = sem("var_done")
        rstd_done = sem("rstd_done")
        xn_done = sem("xn_done")
        xT_ps_done = sem("xT_ps_done")
        xT_hi_done = sem("xT_hi_done")
        xT_lo_done = sem("xT_lo_done")
        wqk_hi_done = sem("wqk_hi_done")
        wqk_lo_done = sem("wqk_lo_done")
        wv_hi_done = sem("wv_hi_done")
        wv_lo_done = sem("wv_lo_done")
        wo_hi_done = sem("wo_hi_done")
        wo_lo_done = sem("wo_lo_done")
        scores_done = sem("scores_done")
        mask_done = sem("mask_done")
        max_done = sem("max_done")
        exp_done = sem("exp_done")
        recip_done = sem("recip_done")
        probs_done = sem("probs_done")
        probsT_ps_done = sem("probsT_ps_done")
        probsT_done = sem("probsT_done")
        v_done = sem("v_done")
        v_copied = sem("v_copied")
        av_done = sem("av_done")
        ao_hi_done = sem("ao_hi_done")
        ao_lo_done = sem("ao_lo_done")
        out_done = sem("out_done")
        out_added = sem("out_added")
        prep_ps_done = sem("prep_ps_done")
        prep_copied = sem("prep_copied")
        cons_done = sem("cons_done")
        kn_done = sem("kn_done")
        kblk_zeroed = sem("kblk_zeroed")
        vblk_ready = sem("vblk_ready")
        xvar_done = sem("xvar_done")
        qfac_done = sem("qfac_done")
        xq_sin = sem("xq_sin")
        xq_cos = sem("xq_cos")
        xq_weighed = sem("xq_weighed")
        xq_done = sem("xq_done")
        xqT_ps_done = sem("xqT_ps_done")
        xqT_copied = sem("xqT_copied")
        xsc_done = sem("xsc_done")
        xmax_done = sem("xmax_done")
        xsub_done = sem("xsub_done")
        xexp_done = sem("xexp_done")
        xsummed = sem("xsummed")
        xrec_done = sem("xrec_done")
        xprobs_done = sem("xprobs_done")
        xpT_ps_done = sem("xpT_ps_done")
        xpT_copied = sem("xpT_copied")
        xav_done = sem("xav_done")
        xao_copied = sem("xao_copied")
        xproj_done = sem("xproj_done")
        x2_done = sem("x2_done")
        fvar_done = sem("fvar_done")
        frstd_done = sem("frstd_done")
        fln_done = sem("fln_done")
        fT_ps_done = sem("fT_ps_done")
        fT_copied = sem("fT_copied")
        logits_done = sem("logits_done")
        fh_done = sem("fh_done")
        fw_hi_done = sem("fw_hi_done")
        fw_lo_done = sem("fw_lo_done")
        fT_hi_done = sem("fT_hi_done")
        fT_lo_done = sem("fT_lo_done")
        fhm_hi_done = sem("fhm_hi_done")
        fhm_lo_done = sem("fhm_lo_done")
        fexp_done = sem("fexp_done")
        onehot_done = sem("onehot_done")
        chosen_done = sem("chosen_done")
        fmask_done = sem("fmask_done")
        fmask_copied = sem("fmask_copied")
        fhm_done = sem("fhm_done")
        y_done = sem("y_done")
        final_done = sem("final_done")
        x_loaded = [sem(f"x_loaded{d}") for d in range(TILES // 2)]
        qk_cos = [sem("q_cos"), sem("k_cos")]
        qk_done = [sem("q_done"), sem("k_done")]
        qk_roped = [sem("q_roped"), sem("k_roped")]
        qk_sin = [sem("q_sin"), sem("k_sin")]
        qk_swapped = [sem("q_swapped"), sem("k_swapped")]
        block = stack.enter_context(nc.Block())

        def C(name, rows=slice(0, P)):
            lo, hi = _COLS[name]
            return cst[rows, lo:hi]

        ident = C("ident")
        split3 = [(0, 0), (0, 1), (1, 0)]
        xT = (xT_hi, xT_lo)
        wqk = (wqk_hi, wqk_lo)
        wv = (wv_hi, wv_lo)
        wo = (wo_hi, wo_lo)
        ao = (ao_hi, ao_lo)
        BQ, BK, BS, BT_, BAV, BW0, BW1, BP = bank

        def needed(value):
            return not isinstance(value, int) or value > 0

        def has(mode, u, lag):
            if mode == "first":
                return u - lag >= 0
            if mode == "last":
                return u - lag < 0
            return True

        def prep_groups():
            groups = [(wxoT[:, :, :].rearrange("p k n -> p (k n)"), P, P,
                       [wst2[:, k, h * P:(h + 1) * P] for h in range(KC) for k in range(KC)]),
                      (wrT[:, :, :].rearrange("p k n -> p (k n)"), P, E, [wr_st[:, k * P:(k + 1) * P] for k in range(KC)])]
            for k in range(KC):
                groups.append((aT[:, k, :], P, P, [xn[:, m, k * P:(k + 1) * P] for m in range(EM)]))
            for m in range(0, EM, 2):
                groups.append((bT[:, m:m + 2, :].rearrange("p m n -> p (m n)"), P, P,
                               [xn[:, 4 + 2 * k:6 + 2 * k, :].rearrange("p t n -> p (t n)")[:, j * P:(j + 1) * P]
                                for j in (m, m + 1) for k in range(KC)]))
            for t in range(0, TILES, CT):
                groups.append((kT[:, :, :].rearrange("p b n -> p (b n)")[:, t * P:(t + CT) * P], XC, P, [cx[:, j, :] for j in range(t, t + CT)]))
            return groups

        PREP = prep_groups()

        SPLITS = ([(aT[:, k, :], aT_hi[:, k, :], aT_lo[:, k, :]) for k in range(KC)] +
                  [(bT[:, m:m + 2, :], bT_hi[:, m:m + 2, :], bT_lo[:, m:m + 2, :]) for m in range(0, EM, 2)])

        @block.sync
        def _(sp):
            def load_x(d):
                sp.dma_start(xr[:, duo(d), :], x_v[:, duo(d), :]).then_inc(x_loaded[d], 16)

            def load_w(i, w):
                sp.dma_start(w_st[:, :, w, :], wqkv_v[:, :, w, bass.ds(i * 2 * HD, 2 * HD)]).then_inc(wv_loaded if w == 2 else wqk_loaded, 16)

            def load_wo(i):
                sp.dma_start(wo_st[:, :, :], wo_v[:, bass.ds(i * 2, 2), :]).then_inc(wo_loaded, 16)

            load_x(0)
            load_x(1)
            sp.dma_start(ident, consts[:, 0:P]).then_inc(ident_loaded, 16)
            load_x(2)
            load_x(3)
            load_w(0, 0)
            load_w(0, 1)
            sp.dma_start(cst[:, P:CONST_N], consts[:, P:CONST_N]).then_inc(consts_loaded, 16)
            load_w(0, 2)
            load_wo(0)
            sp.dma_start(cx[:, :, :], ctx_v).then_inc(ctx_loaded, 16)
            for half in range(2):
                sp.dma_start(cx2[half * S:(half + 1) * S, :, :], ctx_in.rearrange("b s d -> s b d")).then_inc(ctx_loaded, 16)
            small, rows = small_loaded, rows_loaded
            sp.dma_start(kw_bc[:, :], k_norm_w.rearrange("(a n) -> a n", a=1).to_broadcast([P, XC])).then_inc(rows, 16)
            sp.dma_start(qw_bc[:, :], q_norm_w.rearrange("(a n) -> a n", a=1).to_broadcast([P, D])).then_inc(rows, 16)
            sp.dma_start(br_bc[:, :], ffn_br.rearrange("(a n) -> a n", a=1).to_broadcast([P, E])).then_inc(rows, 16)
            sp.dma_start(wr_st[:, :], ffn_wr).then_inc(small, 16)
            sp.dma_start(wst2[:, 0:2, :], wx_o.rearrange("(k p) c -> p k c", p=P)).then_inc(small, 16)
            sp.wait_ge(xT_ps_done, TILES // 2)
            sp.dma_start(xn[:, 0:4, :], ffn_a.rearrange("e r d -> (e r) d").rearrange("(m p) d -> p m d", p=P)).then_inc(ab_loaded, 16)
            for k in range(KC):
                sp.dma_start(xn[:, 4 + 2 * k:6 + 2 * k, :].rearrange("p t (e r) -> p (t e) r", r=R),
                             ffn_b[:, k * P:(k + 1) * P, :].rearrange("e o r -> o e r")).then_inc(ab_loaded, 16)
            with sp.Fori(1, PAIRS) as i:
                sp.wait_ge(wqk_hi_done, i * 2)
                sp.wait_ge(wqk_lo_done, i * 2)
                sp.wait_ge(wv_hi_done, i)
                sp.wait_ge(wv_lo_done, i)
                for w in range(3):
                    load_w(i, w)
                sp.wait_ge(wo_hi_done, i)
                sp.wait_ge(wo_lo_done, i)
                load_wo(i)
            sp.wait_ge(prep_copied, len(PREP))
            for h in range(XH):
                k, hh, g = h // HH, h % HH, h // (XH // XG)
                if hh == 0:
                    sp.wait_ge(kblk_zeroed, (2, 6)[k])
                sp.dma_start(kblk[hh * XD:(hh + 1) * XD, k, :, hh, :], kT[g * XD:(g + 1) * XD, :, :]).then_inc(kblk_loaded, 16)
            for t in range(TILES):
                sp.wait_ge(final_done, t + 1)
                sp.dma_start(out_v[:, t, :], final[:, t, :]).then_inc(out_stored, 16)
            sp.wait_ge(out_stored, 16 * TILES)

        @block.gpsimd
        def _(pool):
            pool.memset(mhalf[:, :], -0.5).then_inc(pool_step, 1)
            pool.memset(kblk[:, 0, 0:12, :, :], 0.0).then_inc(kblk_zeroed, 1)
            pool.wait_ge(pool_step, 1)

            for c in range(CHUNKS):
                pool.wait_ge(var_done, c + 1)
                pool.tensor_tensor(rstd[:, c * CT:(c + 1) * CT], veps[:, c * CT:(c + 1) * CT], mhalf[:, 0:CT], ALU.pow).then_inc(rstd_done, 1)
                if c == 0:
                    pool.memset(kblk[:, 0, 12:B, :, :], 0.0).then_inc(kblk_zeroed, 1)

            def lo_qk(h, it):
                pool.wait_ge(wqk_hi_done, it * 2 + h + 1)
                if needed(it):
                    pool.wait_ge(qk_done[1], it * 4 - 1 + h)
                pool.tensor_tensor(wqk_lo[h][:, :, :, :], w_st[:, :, 0:2, h * HD:(h + 1) * HD], wqk_hi[h][:, :, :, :].bitcast(F32), ALU.subtract).then_inc(wqk_lo_done, 1)

            def lo_v(it):
                pool.wait_ge(wv_hi_done, it + 1)
                pool.tensor_tensor(wv_lo[:, :, :], w_st[:, :, 2, :], wv_hi[:, :, :].bitcast(F32), ALU.subtract).then_inc(wv_lo_done, 1)

            def lo_o(it):
                pool.wait_ge(wo_hi_done, it + 1)
                pool.tensor_tensor(wo_lo[:, :, :], wo_st[:, :, :], wo_hi[:, :, :].bitcast(F32), ALU.subtract).then_inc(wo_lo_done, 1)

            lo_qk(0, 0)
            pool.memset(vblk[:, :, :, :], 0.0).then_inc(vblk_zeroed, 1)

            def prepare_cross(u):
                if u == 0:
                    pool.wait_ge(cssq_done, 1)
                    pool.tensor_tensor(crr[:, :], cssq[:, :], mhalf[:, 0:TILES], ALU.pow).then_inc(crr_done, 1)

            def zero_keys(i):
                pool.memset(kblk[:, 1, i * (B // 4):(i + 1) * (B // 4), :, :], 0.0).then_inc(kblk_zeroed, 1)

            def rope_add(it, u):
                h, n = u % 2, it * 4 + u
                for i in range(2):
                    pool.wait_ge(qk_sin[i], n + 1)
                    if i == 0:
                        if needed(n - 1):
                            pool.wait_ge(scores_done, n - 1)
                    pool.tensor_tensor(qk[h][i][:, :], cos_t[i][:, :], sin_t[i][:, :], ALU.add).then_inc(qk_roped[i], 1)

            def normalise(it, u):
                h, n = (u - 1) % 2, it * 4 + u - 1
                pool.wait_ge(recip_done, n + 1)
                if needed(n - 1):
                    pool.wait_ge(probsT_ps_done, n - 1)
                pool.tensor_tensor(probs[h][:, :, :], expd[h][:, :, :],
                                   rrec[h][:, :].unsqueeze(2).to_broadcast([P, CT, P]), ALU.mult).then_inc(probs_done, 1)

            def iteration(it, mode):
                for u in range(4):
                    if has(mode, u, 0) and mode != "last":
                        if u == 0:
                            lo_qk(1, it)
                            lo_v(it)
                        if u == 3:
                            lo_o(it)
                            if mode != "end":
                                lo_qk(0, it + 1)
                        rope_add(it, u)
                    if has(mode, u, 1):
                        normalise(it, u)
                    if mode == "first":
                        prepare_cross(u)
                    if mode in ("first", "end") and u in (1, 2):
                        zero_keys(u - 1 if mode == "first" else u + 1)

            iteration(0, "first")
            with pool.Fori(1, PAIRS - 1) as it:
                iteration(it, "loop")
            iteration(PAIRS - 1, "end")
            iteration(PAIRS, "last")

            def expert_rstd(d):
                pool.wait_ge(fvar_done, d + 1)
                pool.tensor_tensor(rstd[:, duo(d)], veps[:, duo(d)], mhalf[:, 0:2], ALU.pow).then_inc(frstd_done, 1)

            def inputs_low(d):
                pool.wait_ge(fT_hi_done, d + 1)
                cols = slice((d % 2) * 2 * P, (d % 2 + 1) * 2 * P)
                pool.tensor_tensor(fT_lo[d // 2][:, :, cols], fT[d // 2][:, :, cols], fT_hi[d // 2][:, :, cols].bitcast(F32), ALU.subtract).then_inc(fT_lo_done, 1)

            def query_factor(d):
                pool.wait_ge(xvar_done, d + 1)
                pool.tensor_tensor(qfac[:, duo(d)], fvar[:, duo(d)], mhalf[:, 0:2], ALU.pow).then_inc(qfac_done, 1)

            def query_cosines(d):
                pool.wait_ge(xq_weighed, d + 1)
                pool.tensor_tensor(xcos(d).rearrange("p t (h d) -> p (t h) d", d=XD), xq[:, duo(d), :].rearrange("p t (h d) -> p (t h) d", d=XD),
                                   C("xcosq").unsqueeze(1).to_broadcast([P, 2 * XH, XD]), ALU.mult).then_inc(xq_cos, 1)

            def query_sines(d):
                q4 = xq[:, duo(d), :].rearrange("p t (h f d) -> p (t h) f d", f=2, d=XD // 2)
                o4 = xsin(d).rearrange("p t (h f d) -> p (t h) f d", f=2, d=XD // 2)
                sn = C("xsinq").rearrange("p (f d) -> p f d", f=2)
                for f in range(2):
                    i = pool.tensor_tensor(o4[:, :, f, :], q4[:, :, 1 - f, :],
                                           sn[:, f, :].unsqueeze(1).to_broadcast([P, 2 * XH, XD // 2]), ALU.mult)
                i.then_inc(xq_sin, 1)

            def rotate_queries(d):
                if d >= 2:
                    pool.wait_ge(xq_cos, d - 1)
                pool.wait_ge(xq_sin, d + 1)
                pool.tensor_tensor(xq[:, duo(d), :], xcos(d), xsin(d), ALU.add).then_inc(xq_done, 1)

            query_factor(0)
            rotate_queries(1)
            query_factor(1)
            for v in range(UNITS):
                pool.wait_ge(xrec_done, v + 1)
                if needed(v - 1):
                    pool.wait_ge(xpT_ps_done, v - 1)
                pool.tensor_tensor(xprobs_t[v % 2][:, :, :], xsc_t[v % 4][:, :, :],
                                   xrec_t[v % 2][:, :].unsqueeze(2).to_broadcast([P, HH, S]), ALU.mult).then_inc(xprobs_done, 1)
                if v in (2, 5):
                    query_cosines(2 + v // 5)
                if v in (3, 6):
                    query_sines(2 + v // 6)
                if v in (4, 7):
                    rotate_queries(2 + v // 7)
                    query_factor(2 + v // 7)
                if v in (8, 12, 15):
                    expert_rstd((v - 7) // 4)
                if 9 <= v < 13:
                    whole, hi, lo = SPLITS[v - 9]
                    pool.wait_ge(fw_hi_done, v - 8)
                    pool.tensor_tensor(lo, whole, hi.bitcast(F32), ALU.subtract).then_inc(fw_lo_done, 1)
                if v in (13, 15):
                    inputs_low((v - 13) // 2)
            expert_rstd(3)
            inputs_low(2)
            inputs_low(3)

        @block.scalar
        def _(act):
            def hi_qk(h, it):
                act.wait_ge(wqk_loaded, it * 32 + 32)
                if needed(it):
                    act.wait_ge(qk_done[1], it * 4 - 1 + h)
                    act.wait_ge(wqk_lo_done, it * 2 - 1 + h)
                act.activation(wqk_hi[h][:, :, :, :], w_st[:, :, 0:2, h * HD:(h + 1) * HD], ACT.Copy).then_inc(wqk_hi_done, 1)

            def hi_v(it):
                act.wait_ge(wv_loaded, it * 16 + 16)
                if needed(it):
                    act.wait_ge(v_done, it * 2)
                    act.wait_ge(wv_lo_done, it)
                act.activation(wv_hi[:, :, :], w_st[:, :, 2, :], ACT.Copy).then_inc(wv_hi_done, 1)

            def hi_o(it):
                act.wait_ge(wo_loaded, it * 16 + 16)
                if needed(it):
                    act.wait_ge(out_done, it * 2)
                    act.wait_ge(wo_lo_done, it)
                act.activation(wo_hi[:, :, :], wo_st[:, :, :], ACT.Copy).then_inc(wo_hi_done, 1)

            def tokens_high(d):
                act.wait_ge(xT_ps_done, d + 1)
                act.activation(xT_hi[:, :, d * 2 * P:(d + 1) * 2 * P], bank[XT_BANKS[d]][:, :].rearrange("p (k n) -> p k n", k=KC), ACT.Copy).then_inc(xT_hi_done, 1)

            hi_qk(0, 0)
            tokens_high(0)
            tokens_high(1)

            def place_values():
                act.wait_ge(vblk_zeroed, 1)
                act.wait_ge(ctx_loaded, 48)
                for half in range(2):
                    rows = slice(half * S, (half + 1) * S)
                    act.activation(vblk[rows, :, :, half * XD:(half + 1) * XD],
                                   cx2[rows, :, :].rearrange("p b (g d) -> p b g d", g=XG), ACT.Copy).then_inc(vblk_ready, 1)

            def swap(it, u):
                n = it * 4 + u
                for i, bk in enumerate((BQ, BK)):
                    act.wait_ge(qk_done[i], n + 1)
                    if needed(n):
                        act.wait_ge(qk_sin[i], n)
                    act.activation(swapped[i][0:S, :], bk[S:P, :], ACT.Copy)
                    act.activation(swapped[i][S:P, :], bk[0:S, :], ACT.Copy).then_inc(qk_swapped[i], 1)

            def exponentials(it, u):
                h, n = (u - 1) % 2, it * 4 + u - 1
                act.wait_ge(max_done, n + 1)
                if needed(n - 1):
                    act.wait_ge(probs_done, n - 1)
                for t in range(CT):
                    i = act.activation(expd[h][:, t, :], masked[h][:, t, :], ACT.Exp, bias=nmax[h][:, t:t + 1],
                                       scale=1.0, accum_out=rsum[h][:, t:t + 1])
                i.then_inc(exp_done, 1)

            def copy_probsT(it, u):
                n = it * 4 + u - 2
                act.wait_ge(probsT_ps_done, n + 1)
                if needed(n):
                    act.wait_ge(av_done, n)
                act.activation(probsT[:, :, :], BT_[:, :].rearrange("p (t n) -> p t n", t=CT), ACT.Copy).then_inc(probsT_done, 1)

            def copy_v(it, c):
                act.wait_ge(v_done, it * 2 + c + 1)
                if needed(it):
                    act.wait_ge(av_done, it * 4 - 2 + 2 * c)
                act.activation(vals[c][:, 0:2, :], BW0[:, :].rearrange("p (t n) -> p t n", t=2), ACT.Copy)
                act.activation(vals[c][:, 2:4, :], BW1[:, :].rearrange("p (t n) -> p t n", t=2), ACT.Copy).then_inc(v_copied, 1)

            def ao_high(it, u):
                n, c, h = it * 4 + u - 2, ((u - 2) % 4) // 2, u % 2
                act.wait_ge(av_done, n + 1)
                act.activation(ao_hi[c][h][:, :], BAV[:, :], ACT.Copy).then_inc(ao_hi_done, 1)

            def iteration(it, mode):
                for u in range(4):
                    live = mode != "last"
                    if live and u == 0:
                        hi_qk(1, it)
                        hi_v(it)
                    if live and u == 3:
                        hi_o(it)
                        if mode != "end":
                            hi_qk(0, it + 1)
                    if live:
                        swap(it, u)
                    if mode == "last" and has(mode, u, 1):
                        exponentials(it, u)
                    if has(mode, u, 2):
                        copy_probsT(it, u)
                    if live and has(mode, u, 1):
                        exponentials(it, u)
                    if live and u % 2:
                        copy_v(it, u // 2)
                    if has(mode, u, 2):
                        ao_high(it, u)
                    if mode == "first" and u == 0:
                        tokens_high(2)
                        tokens_high(3)
                        place_values()

            iteration(0, "first")
            with act.Fori(1, PAIRS - 1) as it:
                iteration(it, "loop")
            iteration(PAIRS - 1, "end")
            iteration(PAIRS, "last")

            def copy_qT(d):
                act.wait_ge(xqT_ps_done, d + 1)
                act.activation(qT[:, duo(d), :, :], bank[7 if d < 2 else 5][:, :].rearrange("p (t k n) -> p t k n", t=2, k=KC), ACT.Copy).then_inc(xqT_copied, 1)

            def copy_fT(d):
                act.wait_ge(fT_ps_done, d + 1)
                bk = bank[(5, 4, 4, 6)[d]][:, :].rearrange("p (k n) -> p k n", k=KC)
                cols = slice((d % 2) * 2 * P, (d % 2 + 1) * 2 * P)
                act.activation(fT[d // 2][:, :, cols], bk, ACT.Copy).then_inc(fT_copied, 1)
                act.activation(fT_hi[d // 2][:, :, cols], bk, ACT.Copy).then_inc(fT_hi_done, 1)

            def gate_exp(c):
                act.wait_ge(lshift_done, c + 1)
                act.activation(lg_t[c][:, 2, :], lg_t[c][:, 1, :], ACT.Exp).then_inc(fexp_done, 1)

            copy_qT(0)
            for v in range(UNITS + 3):
                if v == UNITS + 2:
                    gate_exp(0)
                if v >= 3:
                    w = v - 3
                    act.wait_ge(xav_done, w + 1)
                    if needed(w // 2 - 1):
                        act.wait_ge(xproj_done, w // 2 - 1)
                    act.activation(xaoT_t[w // 2 % 2][:, w % 2, :], bank[6][:, (w % 2) * P:(w % 2 + 1) * P], ACT.Copy).then_inc(xao_copied, 1)
                if 2 <= v < UNITS + 2:
                    w = v - 2
                    act.wait_ge(xpT_ps_done, w + 1)
                    if needed(w - 1):
                        act.wait_ge(xav_done, w - 1)
                    act.activation(xpT_t[w % 2][:, :, :], bank[4 + w % 2][:, :].rearrange("p (m n) -> p m n", m=4), ACT.Copy).then_inc(xpT_copied, 1)
                if v < UNITS:
                    act.wait_ge(xsub_done, v + 1)
                    if v % 4 == 0:
                        act.wait_ge(qfac_done, v // 4 + 1)
                    act.activation(xsc_t[v % 4][:, :, :], xsc_t[v % 4][:, :, :], ACT.Exp, scale=qfac[:, v // 2:v // 2 + 1]).then_inc(xexp_done, 1)
                if v in (2, 6, 10):
                    copy_qT(v // 4 + 1)
                if 7 <= v < 11:
                    whole, hi, _ = SPLITS[v - 7]
                    act.wait_ge(prep_copied, 6)
                    act.activation(hi, whole, ACT.Copy).then_inc(fw_hi_done, 1)
                if v in (12, 15):
                    copy_fT((v - 11) // 4)

            for c in range(CHUNKS):
                if c == 1:
                    gate_exp(1)
                act.wait_ge(onehot_done, c + 1)
                if needed(EM * c):
                    act.wait_ge(fmask_done, EM * c)
                act.activation(chosen[:, :].rearrange("p (n r) -> p n r", r=R), onehot[c][:, :].unsqueeze(2).to_broadcast([P, CT * E, R]), ACT.Copy).then_inc(chosen_done, 1)
                if c == 0:
                    copy_fT(2)
                for i, m in enumerate(M_ORDER):
                    act.wait_ge(fmask_done, EM * c + i + 1)
                    if c:
                        act.wait_ge(fhm_done, EM * (c - 1) + i + 1)
                    act.activation(fmask[:, m, :], bank[MASK_BANKS[i]][:, :], ACT.Copy).then_inc(fmask_copied, 1)
                if c == 0:
                    copy_fT(3)
                for i, m in enumerate(M_ORDER):
                    act.wait_ge(fhm_done, EM * c + i + 1)
                    act.activation(fhm_hi[c][:, m, :], fhm[:, m, :], ACT.Copy).then_inc(fhm_hi_done, 1)

        @block.tensor
        def _(pe):
            pe.wait_ge(ident_loaded, 16)
            def transpose_tokens(d):
                for t in range(2):
                    pe.wait_ge(xn_done, 2 * d + t + 1)
                    for k in range(KC):
                        i = pe.transpose(bank[XT_BANKS[d]][:, (2 * k + t) * P:(2 * k + t + 1) * P], xn[:, 2 * d + t, k * P:(k + 1) * P], ident)
                i.then_inc(xT_ps_done, 1)

            transpose_tokens(0)
            transpose_tokens(1)

            def project_qk(it, u, mode):
                c, h, n = u // 2, u % 2, it * 4 + u
                if c == 0:
                    pe.wait_ge(wqk_hi_done, it * 2 + h + 1)
                for i, bk in enumerate((BQ, BK)):
                    if needed(n):
                        pe.wait_ge(qk_cos[i], n)
                    for j, (a, b) in enumerate(split3):
                        if j == 1 and mode == "first" and i == 0:
                            pe.wait_ge(xT_lo_done, 2 * c + 2)
                        if j == 2 and c == 0 and i == 0:
                            pe.wait_ge(wqk_lo_done, it * 2 + h + 1)
                        for k in range(KC):
                            mm = pe.matmul(bk[:, :], wqk[a][h][:, k, i, :], xT[b][:, k, c * CN:(c + 1) * CN],
                                           start=(j == 0 and k == 0), stop=(j == 2 and k == KC - 1))
                    mm.then_inc(qk_done[i], 1)

            def scores(it, u):
                h, n = (u - 1) % 2, it * 4 + u - 1
                pe.wait_ge(qk_roped[1], n + 1)
                if needed(n):
                    pe.wait_ge(mask_done, n)
                for t in range(CT):
                    cols = slice(t * P, (t + 1) * P)
                    mm = pe.matmul(BS[:, cols], qk[h][0][:, cols], qk[h][1][:, cols], start=True, stop=True)
                mm.then_inc(scores_done, 1)

            def transpose_probs(it, u):
                h, n = u % 2, it * 4 + u - 2
                pe.wait_ge(probs_done, n + 1)
                if needed(n):
                    pe.wait_ge(probsT_done, n)
                for t in range(CT):
                    mm = pe.transpose(BT_[:, t * P:(t + 1) * P], probs[h][:, t, :], ident)
                mm.then_inc(probsT_ps_done, 1)

            def attend(it, u):
                h, c, n = u % 2, ((u - 2) % 4) // 2, it * 4 + u - 2
                pe.wait_ge(probsT_done, n + 1)
                pe.wait_ge(v_copied, 2 * it + c + 1 if u >= 2 else 2 * it - 1 + c)
                if needed(n):
                    pe.wait_ge(ao_lo_done, n)
                for t in range(CT):
                    mm = pe.matmul(BAV[:, t * P:(t + 1) * P], vals[c][:, t, h * HD:(h + 1) * HD], probsT[:, t, :], start=True, stop=True)
                mm.then_inc(av_done, 1)

            def project_v(it, c):
                if c == 0:
                    pe.wait_ge(wv_hi_done, it + 1)
                    pe.wait_ge(wv_lo_done, it + 1)
                if needed(2 * it - 1 + c):
                    pe.wait_ge(out_added, 2 * it - 1 + c)
                for t in range(CT):
                    bk = (BW0, BW1)[t // 2]
                    toks = slice((c * CT + t) * P, (c * CT + t + 1) * P)
                    for j, (a, b) in enumerate(split3):
                        for k in range(KC):
                            mm = pe.matmul(bk[:, (t % 2) * D:(t % 2 + 1) * D], xT[a][:, k, toks], wv[b][:, k, :],
                                           start=(j == 0 and k == 0), stop=(j == 2 and k == KC - 1))
                mm.then_inc(v_done, 1)

            def project_out(it, c):
                if c == 0:
                    pe.wait_ge(wo_hi_done, it)
                    pe.wait_ge(wo_lo_done, it)
                if isinstance(it, int) and c == 1:
                    pe.wait_ge(out_added, 2 * it - 1)
                pe.wait_ge(ao_lo_done, it * 4 - 2 + 2 * c)
                for t in range(CT):
                    bk = (BW0, BW1)[t // 2]
                    for j, (a, b) in enumerate(split3):
                        for h in range(2):
                            mm = pe.matmul(bk[:, (t % 2) * D:(t % 2 + 1) * D], ao[a][c][h][:, t * P:(t + 1) * P], wo[b][:, h, :],
                                           start=(j == 0 and h == 0), stop=(j == 2 and h == 1))
                mm.then_inc(out_done, 1)

            def prepare(g):
                if g == 0:
                    pe.wait_ge(small_loaded, 2 * 16)
                if g == 2:
                    pe.wait_ge(ab_loaded, 3 * 16)
                if g == 6:
                    pe.wait_ge(kn_done, 1)
                if needed(g):
                    pe.wait_ge(prep_copied, g)
                _, rows, cols, sources = PREP[g]
                for m, src in enumerate(sources):
                    n = src.shape[0]
                    i = pe.transpose(BP[0:rows, m * cols:(m + 1) * cols], src, ident[0:n, 0:n])
                i.then_inc(prep_ps_done, 1)

            def iteration(it, mode):
                for u in range(4):
                    live = mode != "last"
                    if mode == "first":
                        pe.wait_ge(xT_hi_done, 2 * (u // 2) + 2)
                    if live:
                        project_qk(it, u, mode)
                    if mode == "first" and u == 0:
                        transpose_tokens(2)
                        transpose_tokens(3)
                    if mode == "first":
                        prepare((0, 1, 3, 4)[u])
                    if mode == "end" and u < 2:
                        prepare(6 + u)
                    if has(mode, u, 1):
                        scores(it, u)
                    if mode == "last" and u == 0:
                        pe.wait_ge(v_copied, 2 * it)
                        project_out(it, 0)
                    if has(mode, u, 2):
                        transpose_probs(it, u)
                    if u % 2 and live:
                        project_v(it, u // 2)
                    if u % 2 == 0 and live and mode != "first":
                        pe.wait_ge(v_copied, 2 * it + u // 2)
                        project_out(it, u // 2)
                    if has(mode, u, 2):
                        attend(it, u)
                    if mode == "first" and u % 2:
                        prepare((2, 5)[u // 2])

            iteration(0, "first")
            with pe.Fori(1, PAIRS - 1) as it:
                iteration(it, "loop")
            iteration(PAIRS - 1, "end")
            iteration(PAIRS, "last")

            def queries(d):
                pe.wait_ge(xq_done, d + 1)
                for t in range(2):
                    for k in range(KC):
                        i = pe.transpose(bank[7 if d < 2 else 5][:, t * D + k * P:t * D + (k + 1) * P], xq[:, 2 * d + t, k * P:(k + 1) * P], ident)
                i.then_inc(xqT_ps_done, 1)

            def tokens(d):
                pe.wait_ge(fln_done, d + 1)
                for k in range(KC):
                    for t in range(2):
                        i = pe.transpose(bank[(5, 4, 4, 6)[d]][:, (2 * k + t) * P:(2 * k + t + 1) * P], xn[:, 2 * d + t, k * P:(k + 1) * P], ident)
                i.then_inc(fT_ps_done, 1)

            def cross_scores(w):
                t, k = w // 2, w % 2
                if w % 4 == 0:
                    pe.wait_ge(xqT_copied, w // 4 + 1)
                if needed(w - 3):
                    pe.wait_ge(xsub_done, w - 3)
                bk = bank[w % 4]
                pe.matmul(bk[:, :], identb[:, :], xmaskb[:, :].unsqueeze(1).to_broadcast([P, HH, S]),
                          start=True, stop=False, skip_group_check=True)
                for b in range(2):
                    mm = pe.matmul(bk[b * S:(b + 1) * S, :], qT[:, t, k, b * S:(b + 1) * S],
                                   kblk[:, k, 2 * t + b, :, :], start=False, stop=True, skip_group_check=True)
                mm.then_inc(xsc_done, 1)

            def cross_project(t):
                pe.wait_ge(xao_copied, 2 * t + 2)
                if needed(t):
                    pe.wait_ge(x2_done, t)
                else:
                    pe.wait_ge(xqT_copied, 2)
                for k in range(KC):
                    i = pe.matmul(bank[7][:, 0:D], xaoT_t[t % 2][:, k, :], wxoT[:, k, :], start=(k == 0), stop=(k == KC - 1))
                i.then_inc(xproj_done, 1)

            def logits(c):
                pe.wait_ge(fT_copied, 2 * c + 2)
                if c:
                    pe.wait_ge(fmask_copied, EM)
                for t in range(CT):
                    for k in range(KC):
                        i = pe.matmul(bank[(0, 4)[c]][:, t * E:(t + 1) * E], fT[c][:, k, t * P:(t + 1) * P], wrT[:, k, :], start=(k == 0), stop=(k == KC - 1))
                i.then_inc(logits_done, 1)

            def expand(c, i):
                m = M_ORDER[i]
                if c == 0:
                    pe.wait_ge(xsub_done, UNITS)
                if m == 0 and c == 0:
                    pe.wait_ge(lshift_done, 1)
                if needed(EM * (c - 1) + i + 1):
                    pe.wait_ge(fhm_done, EM * (c - 1) + i + 1)
                pe.wait_ge(fw_lo_done, KC)
                pe.wait_ge(fT_hi_done, 2 * c + 2)
                for j, (a, f) in enumerate(((aT_hi, fT_hi), (aT_lo, fT_hi), (aT_hi, fT_lo))):
                    if j == 2:
                        pe.wait_ge(fT_lo_done, 2 * c + 2)
                    for k in range(KC):
                        mm = pe.matmul(bank[m][:, :], a[:, k, m * P:(m + 1) * P], f[c][:, k, :], start=(j == 0 and k == 0), stop=(j == 2 and k == KC - 1))
                mm.then_inc(fh_done, 1)

            def masks(c):
                pe.wait_ge(chosen_done, c + 1)
                for i, m in enumerate(M_ORDER):
                    if c == 0 and i == 2:
                        pe.wait_ge(x2_done, TILES)
                    if c == 0 and i == 3:
                        pe.wait_ge(fmask_copied, 1)
                    if c == 1 and i == 2:
                        pe.wait_ge(final_done, 2)
                    if c == 1 and i == 3:
                        pe.wait_ge(fmask_copied, EM + 1)
                    for t in range(CT):
                        sel = chosen[:, t * E * R + m * P:t * E * R + (m + 1) * P]
                        mm = pe.matmul(bank[MASK_BANKS[i]][:, t * P:(t + 1) * P], sel, identb[:, :], start=True, stop=True)
                    mm.then_inc(fmask_done, 1)

            def contract(start, end):
                for t in range(start, end):
                    c = t // CT
                    bk = bank[7 - t // 2] if c == 0 else bank[M_ORDER[t - CT]]
                    if c == 1:
                        pe.wait_ge(fhm_done, t + 1)
                    pe.wait_ge(fw_lo_done, len(SPLITS))
                    for j, (f, b) in enumerate(((fhm_hi, bT_hi), (fhm_hi, bT_lo), (fhm_lo, bT_hi))):
                        if j == 2:
                            pe.wait_ge(fhm_lo_done, EM * (c + 1))
                        for i, m in enumerate(M_ORDER):
                            if j == 0:
                                pe.wait_ge(fhm_hi_done, EM * c + i + 1)
                            mm = pe.matmul(bk[:, (t % 2) * D:(t % 2 + 1) * D], f[c][:, m, (t % CT) * P:(t % CT + 1) * P], b[:, m, :],
                                           start=(j == 0 and i == 0), stop=(j == 2 and i == EM - 1))
                    mm.then_inc(y_done, 1)

            queries(0)
            project_out(PAIRS, 1)
            pe.wait_ge(cons_done, 1)
            pe.wait_ge(kblk_loaded, 16 * XH)
            pe.wait_ge(mask_done, 4 * PAIRS)
            cross_scores(0)
            cross_scores(1)
            queries(1)
            cross_scores(2)
            pe.wait_ge(vblk_ready, 2)
            for w in range(UNITS):
                pe.wait_ge(xprobs_done, w + 1)
                if w == 0:
                    pe.wait_ge(ao_lo_done, 4 * PAIRS)
                if needed(w - 1):
                    pe.wait_ge(xpT_copied, w - 1)
                if w in (5, 9):
                    pe.wait_ge(xqT_copied, w // 4 + 2)
                if w in (11, 14):
                    pe.wait_ge(fT_hi_done, (w - 6) // 4)
                for m in range(HH // 2):
                    i = pe.transpose(bank[4 + w % 2][:, m * P:(m + 1) * P],
                                     xprobs_t[w % 2][:, 2 * m:2 * m + 2, :].rearrange("p h n -> p (h n)"), ident)
                i.then_inc(xpT_ps_done, 1)
                if w + 3 < UNITS:
                    cross_scores(w + 3)
                if w in (4, 8):
                    pe.wait_ge(xpT_copied, w)
                    queries(w // 4 + 1)
                if w in (10, 13):
                    pe.wait_ge(xpT_copied, w)
                    tokens((w - 9) // 4)
                if w >= 2 and w % 2 == 0:
                    cross_project(w // 2 - 1)
                if w == UNITS - 2:
                    logits(0)
                if w == UNITS - 1:
                    expand(0, 0)
                t, k = w // 2, w % 2
                pe.wait_ge(xpT_copied, w + 1)
                if w == 0:
                    pe.wait_ge(out_added, 2 * PAIRS)
                if needed(w):
                    pe.wait_ge(xao_copied, w)
                for b in range(2):
                    for m in range(4):
                        i = pe.matmul(bank[6][32 * m:32 * m + 32, k * P + b * S:k * P + (b + 1) * S],
                                      vblk[:, 2 * t + b, 2 * k + m // 2, :], xpT_t[w % 2][:, m, b * S:(b + 1) * S],
                                      start=True, stop=True, tile_position=(0, 32 * m))
                i.then_inc(xav_done, 1)

            expand(0, 1)
            cross_project(TILES - 1)
            tokens(2)
            expand(0, 2)
            pe.wait_ge(fT_hi_done, 3)
            masks(0)
            expand(0, 3)
            tokens(3)
            logits(1)
            contract(0, 2)
            for i in range(EM):
                expand(1, i)
            masks(1)
            contract(2, 4)
            contract(4, 8)

        @block.vector
        def _(dve):
            steps = [0]

            def step(i):
                steps[0] += 1
                i.then_inc(dve_step, 1)
                dve.wait_ge(dve_step, steps[0])

            def token_stats(c):
                for t in range(c * CT, (c + 1) * CT):
                    if t % 2 == 0:
                        dve.wait_ge(x_loaded[t // 2], 16)
                    i = dve.bn_stats(bn6[:, t, :], xr[:, t, :])
                step(i)

            def token_var(c):
                cs = slice(c * CT, (c + 1) * CT)
                for t in range(c * CT, (c + 1) * CT):
                    i = dve.bn_aggr(bn2[:, t, :], bn6[:, t, :])
                step(i)
                dve.tensor_scalar(veps[:, cs], bn2[:, cs, 1], EPS, None, ALU.add).then_inc(var_done, 1)

            def centre(t, src):
                return dve.tensor_scalar(xn[:, t, :], src[:, t, :], bn2[:, t, 0:1], rstd[:, t:t + 1], ALU.subtract, ALU.mult)

            def centre_tokens(c):
                dve.wait_ge(rstd_done, c + 1)
                for t in range(c * CT, (c + 1) * CT):
                    centre(t, xr).then_inc(xn_done, 1)

            def tokens_low(d):
                dve.wait_ge(xT_hi_done, d + 1)
                dve.tensor_tensor(xT_lo[:, :, d * 2 * P:(d + 1) * 2 * P], bank[XT_BANKS[d]][:, :].rearrange("p (k n) -> p k n", k=KC),
                                  xT_hi[:, :, d * 2 * P:(d + 1) * 2 * P].bitcast(F32), ALU.subtract).then_inc(xT_lo_done, 1)

            token_stats(0)
            token_var(0)
            token_stats(1)
            centre_tokens(0)
            token_var(1)
            tokens_low(0)
            tokens_low(1)
            centre_tokens(1)
            dve.wait_ge(consts_loaded, 16)
            dve.tensor_copy(identb[:, :], ident)
            dve.tensor_copy(xmaskb[:, :], C("xmask")).then_inc(cons_done, 1)

            def prepare_keys(u):
                k3, k4 = "p t (g d) -> p (t g) d", "p t (g f d) -> p (t g) f d"
                if u == 0:
                    dve.wait_ge(ctx_loaded, 48)
                    step(dve.tensor_tensor(ks[:, :, :], cx[:, :, :], cx[:, :, :], ALU.mult))
                    step(dve.tensor_reduce(cssq[:, :], ks[:, :, :], AX_X, ALU.add))
                    dve.tensor_scalar(cssq[:, :], cssq[:, :], 1.0 / XC, EPS, ALU.mult, ALU.add).then_inc(cssq_done, 1)
                if u == 1:
                    dve.wait_ge(crr_done, 1)
                    dve.wait_ge(rows_loaded, 48)
                    step(dve.tensor_tensor(ks[:, :, :], cx[:, :, :], crr[:, :].unsqueeze(2).to_broadcast([P, TILES, XC]), ALU.mult))
                    step(dve.tensor_tensor(ks[:, :, :], ks[:, :, :], kw_bc[:, :].unsqueeze(1).to_broadcast([P, TILES, XC]), ALU.mult))
                    ks4, kr4 = ks[:, :, :].rearrange(k4, f=2, d=XD // 2), kr[:, :, :].rearrange(k4, f=2, d=XD // 2)
                    sn = C("xsink").rearrange("p (f d) -> p f d", f=2)
                    for f in range(2):
                        step(dve.tensor_tensor(kr4[:, :, f, :], ks4[:, :, 1 - f, :],
                                               sn[:, f, :].unsqueeze(1).to_broadcast([P, TILES * XG, XD // 2]), ALU.mult))
                if u == 2:
                    step(dve.tensor_tensor(ks[:, :, :].rearrange(k3, d=XD), ks[:, :, :].rearrange(k3, d=XD),
                                           C("xcosk").unsqueeze(1).to_broadcast([P, TILES * XG, XD]), ALU.mult))
                    dve.tensor_tensor(cx[:, :, :], ks[:, :, :], kr[:, :, :], ALU.add).then_inc(kn_done, 1)

            def rope(it, u, i):
                n = it * 4 + u
                bk, cos, sin = (BQ, BK)[i], C(("cosq", "cosk")[i]), C(("sinq", "sink")[i])
                dve.wait_ge(qk_swapped[i], n + 1)
                if needed(n):
                    dve.wait_ge(qk_roped[i], n)
                dve.tensor_tensor(cos_t[i][:, :].rearrange("p (b n) -> p b n", n=S), bk[:, :].rearrange("p (b n) -> p b n", n=S),
                                  cos.unsqueeze(1).to_broadcast([P, CN // S, S]), ALU.mult).then_inc(qk_cos[i], 1)
                dve.tensor_tensor(sin_t[i][:, :].rearrange("p (b n) -> p b n", n=S), swapped[i][:, :].rearrange("p (b n) -> p b n", n=S),
                                  sin.unsqueeze(1).to_broadcast([P, CN // S, S]), ALU.mult).then_inc(qk_sin[i], 1)

            def mask_and_max(it, u):
                h, n = (u - 1) % 2, it * 4 + u - 1
                dve.wait_ge(scores_done, n + 1)
                if needed(n - 1):
                    dve.wait_ge(exp_done, n - 1)
                dve.tensor_tensor(masked[h][:, :, :], BS[:, :].rearrange("p (t n) -> p t n", t=CT),
                                  C("mask").unsqueeze(1).to_broadcast([P, CT, P]), ALU.add).then_inc(mask_done, 1)
                dve.wait_ge(mask_done, n + 1)
                dve.tensor_reduce(nmax[h][:, :], masked[h][:, :, :], AX_X, ALU.max, negate=True).then_inc(max_done, 1)

            def reciprocals(it, u):
                h, n = (u - 1) % 2, it * 4 + u - 1
                dve.wait_ge(exp_done, n + 1)
                if needed(n - 1):
                    dve.wait_ge(probs_done, n - 1)
                dve.reciprocal(rrec[h][:, :], rsum[h][:, :]).then_inc(recip_done, 1)

            def add_out(it, c):
                dve.wait_ge(out_done, 2 * it - 1 + c)
                for k, bk in enumerate((BW0, BW1)):
                    ts = slice(c * CT + 2 * k, c * CT + 2 * k + 2)
                    i = dve.tensor_tensor(xr[:, ts, :], bk[:, :].rearrange("p (t n) -> p t n", t=2), xr[:, ts, :], ALU.add)
                i.then_inc(out_added, 1)

            def ao_low(it, u):
                n, c, h = it * 4 + u - 2, ((u - 2) % 4) // 2, u % 2
                dve.wait_ge(ao_hi_done, n + 1)
                dve.tensor_tensor(ao_lo[c][h][:, :], BAV[:, :], ao_hi[c][h][:, :].bitcast(F32), ALU.subtract).then_inc(ao_lo_done, 1)

            def copy_prepared(g):
                dve.wait_ge(prep_ps_done, g + 1)
                dst, rows, cols, sources = PREP[g]
                dve.tensor_copy(dst, BP[0:rows, 0:cols * len(sources)]).then_inc(prep_copied, 1)

            def iteration(it, mode):
                for u in range(4):
                    live = mode != "last"
                    if live:
                        rope(it, u, 0)
                    if mode == "first" and u > 0:
                        copy_prepared((1, 3, 4)[u - 1])
                    if mode == "end" and u < 2:
                        copy_prepared(6 + u)
                    if has(mode, u, 1):
                        mask_and_max(it, u)
                    if live:
                        rope(it, u, 1)
                    if mode == "first" and u == 0:
                        tokens_low(2)
                        tokens_low(3)
                        copy_prepared(0)
                    if has(mode, u, 1):
                        reciprocals(it, u)
                    if mode == "last" and u == 0:
                        add_out(it, 0)
                        query_part(0, 0)
                        query_part(0, 1)
                    if u % 2 == 0 and live and mode != "first":
                        add_out(it, u // 2)
                    if has(mode, u, 2):
                        ao_low(it, u)
                    if mode == "first" and u % 2:
                        copy_prepared((2, 5)[u // 2])
                    if mode == "first" and u < 3:
                        prepare_keys(u)
                    if mode == "last" and u == 0:
                        query_part(0, 2)
                        query_part(0, 3)
                    if mode == "last" and u == 1:
                        for part in range(4):
                            query_part(1, part)

            def query_part(d, part):
                x3 = "p t (h d) -> p (t h) d"
                x4 = "p t (h f d) -> p (t h) f d"
                if part == 0:
                    dve.wait_ge(out_added, 2 * PAIRS - 1 + d // 2)
                    for t in range(2 * d, 2 * d + 2):
                        i = dve.bn_stats(bn6[:, t, :], xr[:, t, :])
                    step(i)
                    for t in range(2 * d, 2 * d + 2):
                        i = dve.bn_aggr(bn2[:, t, :], bn6[:, t, :])
                    step(i)
                    dve.tensor_scalar(fvar[:, duo(d)], bn2[:, duo(d), 1], 1.0 + EPS, EPS * EPS, ALU.mult, ALU.add).then_inc(xvar_done, 1)
                if part == 1:
                    for t in range(2 * d, 2 * d + 2):
                        i = dve.scalar_tensor_tensor(out=xq[:, t, :], in0=xr[:, t, :], scalar=bn2[:, t, 0:1],
                                                     in1=qw_bc[:, :], op0=ALU.subtract, op1=ALU.mult)
                    i.then_inc(xq_weighed, 1)
                if part == 2:
                    dve.wait_ge(xq_weighed, d + 1)
                    dve.tensor_tensor(xcos(d).rearrange(x3, d=XD), xq[:, duo(d), :].rearrange(x3, d=XD),
                                      C("xcosq").unsqueeze(1).to_broadcast([P, 2 * XH, XD]), ALU.mult)
                if part == 3:
                    dve.wait_ge(xq_weighed, d + 1)
                    q4, o4 = xq[:, duo(d), :].rearrange(x4, f=2, d=XD // 2), xsin(d).rearrange(x4, f=2, d=XD // 2)
                    sn = C("xsinq").rearrange("p (f d) -> p f d", f=2)
                    for f in range(2):
                        i = dve.tensor_tensor(o4[:, :, f, :], q4[:, :, 1 - f, :],
                                              sn[:, f, :].unsqueeze(1).to_broadcast([P, 2 * XH, XD // 2]), ALU.mult)
                    i.then_inc(xq_sin, 1)
                    if d == 0:
                        dve.wait_ge(xq_sin, 1)
                        dve.tensor_tensor(xq[:, duo(0), :], xcos(0), xsin(0), ALU.add).then_inc(xq_done, 1)

            def expert_stats(d):
                dve.wait_ge(x2_done, 2 * d + 2)
                for t in range(2 * d, 2 * d + 2):
                    i = dve.bn_stats(bn6[:, t, :], xr[:, t, :])
                step(i)
                for t in range(2 * d, 2 * d + 2):
                    i = dve.bn_aggr(bn2[:, t, :], bn6[:, t, :])
                step(i)
                dve.tensor_scalar(veps[:, duo(d)], bn2[:, duo(d), 1], EPS, None, ALU.add).then_inc(fvar_done, 1)

            def expert_centre(d):
                dve.wait_ge(frstd_done, d + 1)
                for t in range(2 * d, 2 * d + 2):
                    i = centre(t, xr)
                i.then_inc(fln_done, 1)

            iteration(0, "first")
            with dve.Fori(1, PAIRS - 1) as it:
                iteration(it, "loop")
            iteration(PAIRS - 1, "end")
            iteration(PAIRS, "last")

            def residual(t):
                dve.wait_ge(xproj_done, t + 1)
                dve.tensor_tensor(xr[:, t, :], bank[7][:, 0:D], xr[:, t, :], ALU.add).then_inc(x2_done, 1)

            add_out(PAIRS, 1)

            for v in range(UNITS + 1):
                if v < UNITS:
                    dve.wait_ge(xsc_done, v + 1)
                    dve.tensor_reduce(xmx_t[v % 2][:, :], bank[v % 4][:, :].rearrange("p (h n) -> p h n", n=S), AX_X, ALU.max).then_inc(xmax_done, 1)
                if v >= 1:
                    dve.wait_ge(xexp_done, v)
                    dve.tensor_reduce(xsm_t[(v - 1) % 2][:, :], xsc_t[(v - 1) % 4][:, :, :], AX_X, ALU.add).then_inc(xsummed, 1)
                if v < UNITS:
                    dve.wait_ge(xmax_done, v + 1)
                    if needed(v - 3):
                        dve.wait_ge(xprobs_done, v - 3)
                    dve.tensor_tensor(xsc_t[v % 4][:, :, :], bank[v % 4][:, :].rearrange("p (h n) -> p h n", n=S),
                                      xmx_t[v % 2][:, :].unsqueeze(2).to_broadcast([P, HH, S]), ALU.subtract).then_inc(xsub_done, 1)
                if v >= 1:
                    dve.wait_ge(xsummed, v)
                    if needed(v - 2):
                        dve.wait_ge(xprobs_done, v - 2)
                    dve.reciprocal(xrec_t[(v - 1) % 2][:, :], xsm_t[(v - 1) % 2][:, :]).then_inc(xrec_done, 1)
                if v in (2, 3, 5, 6):
                    query_part(2 + v // 5, (v - 2) % 3)
                if v >= 5 and v % 2:
                    residual((v - 5) // 2)
                if v in (8, 12, 16):
                    expert_stats((v - 7) // 4)
                if v in (10, 14):
                    expert_centre((v - 9) // 4)

            def gate_shift(c):
                lg, lgs = lg_t[c], lgs_t[c]
                dve.wait_ge(logits_done, c + 1)
                step(dve.tensor_tensor(lg[:, 0, :].rearrange("p (t e) -> p t e", e=E), bank[(0, 4)[c]][:, 0:CT * E].rearrange("p (t e) -> p t e", e=E),
                                       br_bc[:, :].unsqueeze(1).to_broadcast([P, CT, E]), ALU.add))
                step(dve.tensor_reduce(lgs[:, 0, :], lg[:, 0, :].rearrange("p (t e) -> p t e", e=E), AX_X, ALU.max))
                dve.tensor_tensor(lg[:, 1, :].rearrange("p (t e) -> p t e", e=E), lg[:, 0, :].rearrange("p (t e) -> p t e", e=E),
                                  lgs[:, 0, :].unsqueeze(2).to_broadcast([P, CT, E]), ALU.subtract).then_inc(lshift_done, 1)

            def choose(c):
                lg, lgs = lg_t[c], lgs_t[c]

                def row(i):
                    return lg[:, i, :].rearrange("p (t e) -> p t e", e=E)

                def bc(i):
                    return lgs[:, i, :].unsqueeze(2).to_broadcast([P, CT, E])

                dve.wait_ge(fexp_done, c + 1)
                step(dve.tensor_reduce(lgs[:, 1, :], row(2), AX_X, ALU.add))
                step(dve.reciprocal(lgs[:, 2, :], lgs[:, 1, :]))
                step(dve.tensor_tensor(row(3), row(2), bc(2), ALU.mult))
                step(dve.tensor_reduce(lgs[:, 3, :], row(3), AX_X, ALU.max))
                step(dve.tensor_scalar(wgt[c][:, :], lgs[:, 3, :], 1.0 / R, None, ALU.mult))
                step(dve.tensor_tensor(row(4), row(3), bc(3), ALU.is_equal))
                step(dve.tensor_tensor(row(5), row(4), C("first").unsqueeze(1).to_broadcast([P, CT, E]), ALU.mult))
                step(dve.tensor_reduce(lgs[:, 4, :], row(5), AX_X, ALU.max))
                dve.tensor_tensor(onehot[c][:, :].rearrange("p (t e) -> p t e", e=E), row(5), bc(4), ALU.is_equal).then_inc(onehot_done, 1)

            def mask_inner(c):
                for i, m in enumerate(M_ORDER):
                    dve.wait_ge(fmask_copied, EM * c + i + 1)
                    dve.wait_ge(fh_done, EM * c + i + 1)
                    if c:
                        dve.wait_ge(fhm_hi_done, EM * (c - 1) + i + 1)
                    dve.tensor_tensor(fhm[:, m, :], bank[m][:, :], fmask[:, m, :], ALU.mult).then_inc(fhm_done, 1)
                for i, m in enumerate(M_ORDER):
                    dve.wait_ge(fhm_hi_done, EM * c + i + 1)
                    dve.tensor_tensor(fhm_lo[c][:, m, :], fhm[:, m, :], fhm_hi[c][:, m, :].bitcast(F32), ALU.subtract).then_inc(fhm_lo_done, 1)

            residual(TILES - 2)
            expert_centre(2)
            gate_shift(0)
            choose(0)
            residual(TILES - 1)
            expert_stats(3)
            expert_centre(3)
            def finish(start, end):
                for t in range(start, end):
                    c = t // CT
                    dve.wait_ge(y_done, t + 1)
                    if t in (0, 2):
                        dve.wait_ge(y_done, t + 2)
                    bk = bank[7 - t // 2] if t < CT else bank[M_ORDER[t - CT]]
                    dve.scalar_tensor_tensor(out=final[:, t, :], in0=bk[:, (t % 2) * D:(t % 2 + 1) * D],
                                             scalar=wgt[c][:, t % CT:t % CT + 1], in1=xr[:, t, :], op0=ALU.mult, op1=ALU.add).then_inc(final_done, 1)

            mask_inner(0)
            gate_shift(1)
            choose(1)
            finish(0, 2)
            mask_inner(1)
            finish(2, 8)


_INS = ["x", "ctx_512", "L0_attn_w_qkv", "L0_attn_w_out", "L0_xattn_q_norm_w", "L0_xattn_k_norm_w", "L0_xattn_w_out",
        "L0_ffn_A", "L0_ffn_B", "L0_ffn_Wr", "L0_ffn_br"]


def kernel(**inputs):
    import concourse.bacc as _bacc
    from concourse.bass_utils import run_bass_kernel_spmd as _run

    nc = _bacc.Bacc("TRN2", target_bir_lowering=False, num_devices=1)
    arrays = {f"in_{name}": np.ascontiguousarray(inputs[name]) for name in _INS}
    arrays["in_constants"] = constants()
    args = [nc.dram_tensor(n, a.shape, mybir.dt.from_np(a.dtype), kind="ExternalInput").ap() for n, a in arrays.items()]
    args.append(nc.dram_tensor("out", (B, S, D), F32, kind="ExternalOutput").ap())
    decoder_kernel(nc, *args)
    r = _run(nc, [arrays], core_ids=[0])
    return r.results[0]["out"]
```
